# Optimizing a Trainium2 kernel written in Bass

```python
import numpy as np
import jax
import jax.numpy as jnp

def _softmax(x, axis=-1):
    return jax.nn.softmax(x, axis=axis)

def _gelu(x):
    return jax.nn.gelu(x, approximate=True)

def _silu(x):
    return jax.nn.silu(x)

def _sigmoid(x):
    return jax.nn.sigmoid(x)

def _layernorm(x, axis=-1, eps=1e-05):
    m = jnp.mean(x, axis=axis, keepdims=True)
    v = jnp.var(x, axis=axis, keepdims=True)
    return (x - m) / jnp.sqrt(v + eps)

def _scatter_add(tgt, idx, src, axis=0):
    return tgt.at[idx].add(src)

def _segment_sum(src, seg, n):
    return jax.ops.segment_sum(src, seg, n)
kernel_name = 'mk_prb_d1_jaxref_r2_6b548a'

def setup_inputs(seed: int=0):
    np.random.seed(seed)
    _w = jnp.asarray

    def _L0_attn_setup():
        import jax, jax.numpy as jnp
        import numpy as np
        N, B, C = (144, 64, 512)
        H = 16
        P_PER_TASK = 4
        NUM_TASKS = 7

        def _prompt_mask(n, p, num_tasks, dtype):
            P = (num_tasks + 1) * p
            r = jnp.arange(n)[:, None]
            c = jnp.arange(n)[None, :]
            blocked = (c < P) & ~((r < P) & (r >= c // p * p))
            return jnp.where(blocked, -jnp.inf, 0.0).astype(dtype)
        key = jax.random.key(seed)
        k1, k2, k3 = jax.random.split(key, 3)
        x = jax.random.normal(k1, (N, B, C), dtype=jnp.float32)
        Wqkv = jax.random.normal(k2, (3 * C, C), dtype=jnp.float32) * 0.02
        bqkv = jnp.zeros((3 * C,), dtype=jnp.float32)
        Wproj = jax.random.normal(k3, (C, C), dtype=jnp.float32) * 0.02
        bproj = jnp.zeros((C,), dtype=jnp.float32)
        return {'x': x, 'Wqkv': Wqkv, 'bqkv': bqkv, 'Wproj': Wproj, 'bproj': bproj}
    _L0_attn_in = _L0_attn_setup()

    def _L0_ffn_setup():
        import jax, jax.numpy as jnp
        import numpy as np
        FP8_MAX = 448.0
        SCALE = 1.0
        _FP8_DTYPE = getattr(jnp, 'float8_e4m3fn', jnp.float16)

        def quantize_e4m3(t, scale):
            return jnp.clip(t / scale, -FP8_MAX, FP8_MAX).astype(_FP8_DTYPE)
        key = jax.random.key(seed)
        kx, kw = jax.random.split(key)
        B, N, C, F = (8, 2048, 512, 512)
        x = jax.random.normal(kx, (B, N, C), dtype=jnp.float32)
        weight = jax.random.normal(kw, (F, C), dtype=jnp.float32) * 0.02
        bias = jnp.zeros((F,), dtype=jnp.float32)
        return {'x': x, 'weight': weight, 'bias': bias}
    _L0_ffn_in = _L0_ffn_setup()
    _d = {'L0_attn_x': _L0_attn_in['x'], 'L0_attn_Wqkv': _L0_attn_in['Wqkv'], 'L0_attn_bqkv': _L0_attn_in['bqkv'], 'L0_attn_Wproj': _L0_attn_in['Wproj'], 'L0_attn_bproj': _L0_attn_in['bproj'], 'L0_ffn_weight': _L0_ffn_in['weight'], 'L0_ffn_bias': _L0_ffn_in['bias']}
    _x0 = _d['L0_attn_x']
    _d['L0_attn_x'] = jax.random.normal(jax.random.fold_in(jax.random.key(seed), 1), (8, 2048, 512), dtype=_x0.dtype)
    del _x0
    return _d

def reference(L0_attn_x, L0_attn_Wqkv, L0_attn_bqkv, L0_attn_Wproj, L0_attn_bproj, L0_ffn_weight, L0_ffn_bias):

    def _L0_attn_ref(x, Wqkv, bqkv, Wproj, bproj):
        import jax, jax.numpy as jnp
        import numpy as np
        N, B, C = (144, 64, 512)
        H = 16
        P_PER_TASK = 4
        NUM_TASKS = 7

        def _prompt_mask(n, p, num_tasks, dtype):
            P = (num_tasks + 1) * p
            r = jnp.arange(n)[:, None]
            c = jnp.arange(n)[None, :]
            blocked = (c < P) & ~((r < P) & (r >= c // p * p))
            return jnp.where(blocked, -jnp.inf, 0.0).astype(dtype)
        n, b, ch = x.shape
        hd = ch // H
        scale = hd ** (-0.5)
        qkv = x @ Wqkv.T + bqkv
        q, k, v = jnp.split(qkv, 3, axis=-1)
        to_heads = lambda t: t.reshape(n, b * H, hd).transpose(1, 0, 2)
        q, k, v = (to_heads(q), to_heads(k), to_heads(v))
        mask = _prompt_mask(n, P_PER_TASK, NUM_TASKS, x.dtype)
        scores = mask + scale * jnp.einsum('bnd,bmd->bnm', q, k)
        attn = jax.nn.softmax(scores, axis=-1)
        out = jnp.einsum('bnm,bmd->bnd', attn, v)
        out = out.transpose(1, 0, 2).reshape(n, b, ch)
        return out @ Wproj.T + bproj

    def _L0_ffn_ref(x, weight, bias):
        import jax, jax.numpy as jnp
        import numpy as np
        FP8_MAX = 448.0
        SCALE = 1.0
        _FP8_DTYPE = getattr(jnp, 'float8_e4m3fn', jnp.float16)

        def quantize_e4m3(t, scale):
            return jnp.clip(t / scale, -FP8_MAX, FP8_MAX).astype(_FP8_DTYPE)
        B, N, C = x.shape
        x2d = x.reshape(B * N, C)
        x_mat = quantize_e4m3(x2d, SCALE).astype(jnp.float16)
        w_mat = quantize_e4m3(weight, SCALE).astype(jnp.float16)
        out2d = (x_mat @ w_mat.T).astype(jnp.float32) * (SCALE * SCALE)
        out2d = out2d + bias
        return out2d.reshape(B, N, -1)
    x = L0_attn_x
    xn = _layernorm(x, axis=-1)
    x = x + _L0_attn_ref(xn, L0_attn_Wqkv, L0_attn_bqkv, L0_attn_Wproj, L0_attn_bproj) + _L0_ffn_ref(xn, L0_ffn_weight, L0_ffn_bias)
    return x

_drawn_inputs = setup_inputs


def setup_inputs(seed=0):
    import zlib

    import numpy as np

    out = dict(_drawn_inputs(seed))
    spreads = {'L0_attn_bqkv': (0.0, 0.1), 'L0_attn_bproj': (0.0, 0.1), 'L0_ffn_bias': (0.0, 0.1)}
    factors = {}
    for name, (base, spread) in spreads.items():
        noise = np.random.default_rng([zlib.crc32(name.encode()), seed]).standard_normal(out[name].shape)
        drawn = base * np.exp(spread * noise) if base else spread * noise
        out[name] = jnp.asarray(drawn.astype(out[name].dtype))
    for name, factor in factors.items():
        out[name] = (out[name] * factor).astype(out[name].dtype)
    return out
```

```python
from contextlib import ExitStack

import concourse.bass as bass
from concourse import mybir

F32 = mybir.dt.float32
F16 = mybir.dt.float16
BF16 = mybir.dt.bfloat16
FP8 = mybir.dt.float8e4
I32 = mybir.dt.int32
ALU = mybir.AluOpType
ACT = mybir.ActivationFunctionType
AX_X = mybir.AxisListType.X

P = 128
N = 8
B = 2048
C = 512
H = 16
D = C // H
KC = C // P
QKV = 3 * C
EPS = 1e-5
PROMPT = 4
TILES = N * B // P
PAIR = 2 * N
QUAD = 4 * C
UNITS = 12
FP8_MAX = 448.0
CHIP_FP8_MAX = 240.0

L_STATS, L_NORM, L_TRANS, L_QKV, L_RES, L_QK, L_SOFT, L_PV, L_SUM, L_PROJ, L_OUT, L_STORE = \
    2, 3, 4, 5, 6, 9, 10, 11, 12, 13, 14, 15


def units_before(n):
    g, r = n // N, n % N
    return UNITS * g + r + max(0, r - 4)


def row_units(n):
    return [(units_before(n) + q, 4 * q) for q in range(1 if n % N < PROMPT else 2)]


def tile_count(i, n):
    return i * PAIR + (n + 1)


def unit_count(i, u):
    return i * (2 * UNITS) + (u + 1)


def after(eng, sem, count):
    if not isinstance(count, int) or count > 0:
        eng.wait_ge(sem, count)


def live(i, j, lag):
    return not isinstance(i, int) or 0 <= i * PAIR + j - lag < TILES


def run_slots(eng, slot):
    for j in range(PAIR):
        slot(0, j)
    with eng.Fori(1, TILES // PAIR) as i:
        for j in range(PAIR):
            slot(i, j)
    for j in range(PAIR):
        slot(TILES // PAIR, j)


def attention_and_fp8_linear(nc, x, Wqkv, bqkv, Wproj, bproj, Wffn, bffn, out):
    x_v = x.rearrange("n (i two b) c -> n i two b c", two=2, b=P)
    out_v = out.rearrange("n (i two b) c -> n i two b c", two=2, b=P)

    with ExitStack() as ctx:
        def sb(name, shape, dt):
            return ctx.enter_context(nc.sbuf_tensor(name, shape, dt))

        def bank(name):
            return ctx.enter_context(nc.psum_tensor(name, [P, 512], F32))

        def sem(name):
            return ctx.enter_context(nc.semaphore(name))

        wqkv_hi = sb("wqkv_hi", [P, KC, QKV], F16)
        wqkv_lo = sb("wqkv_lo", [P, KC, QKV], F16)
        wproj_hi = sb("wproj_hi", [P, KC, C], F16)
        wproj_lo = sb("wproj_lo", [P, KC, C], F16)
        wffn_q = sb("wffn_q", [P, KC, C], BF16)
        bias_rows = sb("bias_rows", [P, QKV], BF16)
        ones = sb("ones", [P, P], BF16)
        ident = sb("ident", [P, P], F32)
        out_bias = sb("out_bias", [P, C], F32)
        amax = sb("amax", [P, 4], F32)
        scale = sb("scale", [P, 2], F32)
        unscale = sb("unscale", [P, 2], F32)
        exponent = sb("exponent", [P, 2], I32)
        exp_scale = sb("exp_scale", [P, 1], F32)
        out_scale = sb("out_scale", [P, 1], F32)
        minus_half = sb("minus_half", [P, 1], F32)

        xs = sb("xs", [P, PAIR, C], F32)
        stats = sb("stats", [P, 2, 6], F32)
        mean_var = sb("mean_var", [P, 2, 2], F32)
        var_eps = sb("var_eps", [P, 2], F32)
        rstd = sb("rstd", [P, 2], F32)
        xn = sb("xn", [P, C], F32)
        xT_hi = sb("xT_hi", [P, 2, C], F16)
        xT_lo = sb("xT_lo", [P, 2, C], F16)
        xT_q = sb("xT_q", [P, 2, C], FP8)
        kv = sb("kv", [P, 2, 2, N, C], F32)
        q = sb("q", [P, N, C], F32)
        linear16 = sb("linear16", [P, 2, C], F16)
        prod_qk = sb("prod_qk", [P, QUAD], F32)
        scores = sb("scores", [P, N * H], F32)
        row_max = sb("row_max", [P, H], F32)
        shifted = sb("shifted", [P, N * H], F32)
        exps = sb("exps", [P, N * H], F32)
        row_sum = sb("row_sum", [P, H], F32)
        inv_sum = sb("inv_sum", [P, H], F32)
        probs = sb("probs", [P, 2, N * H], F32)
        prod_pv = sb("prod_pv", [P, 2, QUAD], F32)
        halves = sb("halves", [P, 4, QUAD // 2], F32)
        oT_hi = sb("oT_hi", [P, C], F16)
        oT_lo = sb("oT_lo", [P, C], F16)

        xT_ps, oT_ps, q_ps, k_ps, v_ps, lin_ps, proj_ps = (
            bank(n) for n in ("xT_ps", "oT_ps", "q_ps", "k_ps", "v_ps", "lin_ps", "proj_ps"))

        scratch = kv[:, :, :, :, :].rearrange("p a b m c -> p (a b m c)")
        wqkv_nat = scratch[:, 0:6144].rearrange("p (j c) -> p j c", c=C)
        wproj_nat = scratch[:, 6144:8192].rearrange("p (j c) -> p j c", c=C)
        wffn_nat = scratch[:, 8192:10240]
        q_small = scratch[:, 15360:15872].bitcast(FP8)
        q_large = scratch[:, 15872:16384].bitcast(FP8)
        is_large = scratch[:, 10240:12288]
        half_w = scratch[:, 12288:14336]
        bqkv_nat = halves[:, 3, 0:QKV // P]
        bias_row = prod_pv[0:1, 0, 0:QKV]
        bias_rest = prod_pv[0:1, 1, 0:QKV]
        bias_mid = halves[0:1, 0, 0:QKV // 2].bitcast(BF16)
        bias_low = halves[0:1, 1, 0:QKV // 2].bitcast(BF16)
        bffn_all = halves[:, 2, 0:C]

        wqkv_loaded = sem("wqkv_loaded")
        wproj_loaded = sem("wproj_loaded")
        wffn_loaded = sem("wffn_loaded")
        bqkv_loaded = sem("bqkv_loaded")
        biases_loaded = sem("biases_loaded")
        bias_row_loaded = sem("bias_row_loaded")
        consts_set = sem("consts_set")
        ident_ready = sem("ident_ready")
        amax_steps = sem("amax_steps")
        amax_parts = sem("amax_parts")
        amax_ready = sem("amax_ready")
        scale_steps = sem("scale_steps")
        scales_ready = sem("scales_ready")
        bias_steps = sem("bias_steps")
        bias_split = sem("bias_split")
        bias_moved = sem("bias_moved")
        out_bias_ready = sem("out_bias_ready")
        quant_steps = sem("quant_steps")
        wffn_quantised = sem("wffn_quantised")
        w_transposed = sem("w_transposed")
        w_hi_ready = sem("w_hi_ready")
        w_ready = sem("w_ready")

        x_loaded = [sem(f"x_loaded{k}") for k in range(PAIR)]
        y_stored = [sem(f"y_stored{k}") for k in range(PAIR)]
        stat_steps = sem("stat_steps")
        var_ready = sem("var_ready")
        rstd_ready = sem("rstd_ready")
        xn_ready = sem("xn_ready")
        xT_ready = sem("xT_ready")
        x_hi_q_ready = sem("x_hi_q_ready")
        x_lo_ready = sem("x_lo_ready")
        q_summed, k_summed, v_summed, lin_summed = (
            sem(n) for n in ("q_summed", "k_summed", "v_summed", "lin_summed"))
        q_kept, k_kept, v_kept, lin_rounded = (
            sem(n) for n in ("q_kept", "k_kept", "v_kept", "lin_rounded"))
        res_step = sem("res_step")
        res_ready = sem("res_ready")
        qk_multiplied = sem("qk_multiplied")
        qk_reduced = sem("qk_reduced")
        max_ready = sem("max_ready")
        shifted_ready = sem("shifted_ready")
        exps_ready = sem("exps_ready")
        sum_steps = sem("sum_steps")
        probs_ready = sem("probs_ready")
        pv_multiplied = sem("pv_multiplied")
        pv_halved = sem("pv_halved")
        oT_ready = sem("oT_ready")
        o_hi_ready = sem("o_hi_ready")
        o_lo_ready = sem("o_lo_ready")
        proj_summed = sem("proj_summed")
        y_ready = sem("y_ready")

        N_BANKS = 20

        def weight_bank(w):
            return (q_ps, k_ps)[w % 2]

        def weight_place(w):
            if w < 12:
                return w % KC, (w // KC) * 512
            return (w - 12) % KC, 0

        block = ctx.enter_context(nc.Block())

        @block.sync
        def _(sp):
            sp.dma_start(wqkv_nat, Wqkv.rearrange("(j p) c -> p j c", p=P)).then_inc(wqkv_loaded, 16)
            sp.dma_start(wffn_nat.rearrange("p (j c) -> p j c", c=C),
                         Wffn.rearrange("(j p) c -> p j c", p=P)).then_inc(wffn_loaded, 16)
            sp.dma_start(wproj_nat, Wproj.rearrange("(j p) c -> p j c", p=P)).then_inc(wproj_loaded, 16)
            sp.dma_start(bqkv_nat, bqkv.rearrange("(p j) -> p j", p=P)).then_inc(bqkv_loaded, 16)
            sp.dma_start(bias_row, bqkv.rearrange("(a n) -> a n", a=1)).then_inc(bias_row_loaded, 16)
            sp.dma_start(out_bias[:, :], bproj.partition_broadcast(P)).then_inc(biases_loaded, 16)
            sp.dma_start(bffn_all, bffn.partition_broadcast(P)).then_inc(biases_loaded, 16)

            def slot(i, j):
                if isinstance(i, int) and (i, j) == (0, 4):
                    sp.wait_ge(bias_split, 1)
                    sp.dma_start(bias_rows[1:2, :], bias_mid).then_inc(bias_moved, 16)
                    sp.dma_start(bias_rows[2:3, :], bias_low).then_inc(bias_moved, 16)
                if live(i, j, 0):
                    after(sp, y_stored[j], i * 16)
                    sp.dma_start(xs[:, j, :], x_v[j % N, i, j // N]).then_inc(x_loaded[j], 16)
                if live(i, j, L_STORE):
                    n = j - L_STORE
                    after(sp, y_ready, tile_count(i, n))
                    sp.dma_start(out_v[n % N, i + n // PAIR, (n // N) % 2],
                                 xs[:, n % PAIR, :]).then_inc(y_stored[n % PAIR], 16)

            run_slots(sp, slot)
            for k in range(PAIR):
                sp.wait_ge(y_stored[k], 16 * (TILES // PAIR))

        @block.gpsimd
        def _(pool):
            nc.gpsimd.memset(ident[:, :], 0.0).then_inc(consts_set, 1)
            pool.wait_ge(consts_set, 1)
            nc.gpsimd.affine_select(out=ident[:, :], in_=ident[:, :], compare_op=ALU.not_equal, fill=1.0,
                                    base=0, pattern=[[-1, P]], channel_multiplier=1).then_inc(ident_ready, 1)
            nc.gpsimd.memset(ones[:, :], 1.0).then_inc(consts_set, 1)
            nc.gpsimd.memset(minus_half[:, :], -0.5).then_inc(consts_set, 1)
            nc.gpsimd.memset(bias_rows[:, :], 0.0).then_inc(consts_set, 1)
            pool.wait_ge(biases_loaded, 32)
            nc.gpsimd.tensor_tensor(out_bias[:, :], out_bias[:, :], bffn_all, ALU.add).then_inc(out_bias_ready, 1)
            pool.wait_ge(amax_parts, 1)
            nc.gpsimd.partition_all_reduce(amax[:, 2:4], amax[:, 0:2], P,
                                           bass.bass_isa.ReduceOp.max).then_inc(amax_ready, 1)
            pool.wait_ge(bias_row_loaded, 16)
            pool.wait_ge(scales_ready, 1)
            pool.wait_ge(consts_set, 4)
            nc.gpsimd.tensor_scalar(bias_row, bias_row, scale[0:1, 0:1], 1.0, ALU.mult, ALU.mult).then_inc(bias_steps, 1)
            pool.wait_ge(bias_steps, 1)
            nc.gpsimd.tensor_copy(bias_rows[0:1, :], bias_row).then_inc(bias_steps, 1)
            pool.wait_ge(bias_steps, 2)
            nc.gpsimd.tensor_tensor(bias_rest, bias_row, bias_rows[0:1, :], ALU.subtract).then_inc(bias_steps, 1)
            pool.wait_ge(bias_steps, 3)
            nc.gpsimd.tensor_copy(bias_mid, bias_rest).then_inc(bias_steps, 1)
            pool.wait_ge(bias_steps, 4)
            nc.gpsimd.tensor_tensor(bias_rest, bias_rest, bias_mid, ALU.subtract).then_inc(bias_steps, 1)
            pool.wait_ge(bias_steps, 5)
            nc.gpsimd.tensor_copy(bias_low, bias_rest).then_inc(bias_split, 1)

            def slot(i, j):
                if live(i, j, L_NORM):
                    n = j - L_NORM
                    after(pool, var_ready, tile_count(i, n))
                    after(pool, xn_ready, tile_count(i, n - 2))
                    nc.gpsimd.tensor_tensor(rstd[:, n % 2:n % 2 + 1], var_eps[:, n % 2:n % 2 + 1],
                                            minus_half[:, :], ALU.pow).then_inc(rstd_ready, 1)
                if live(i, j, L_RES):
                    n = j - L_RES
                    xt = xs[:, n % PAIR, :]
                    if isinstance(i, int) and (i, n) == (0, 0):
                        pool.wait_ge(out_bias_ready, 1)
                    after(pool, xn_ready, tile_count(i, n))
                    nc.gpsimd.tensor_tensor(xt, xt, out_bias[:, :], ALU.add).then_inc(res_step, 1)
                    after(pool, res_step, tile_count(i, n))
                    after(pool, lin_rounded, tile_count(i, n))
                    nc.gpsimd.tensor_tensor(xt, xt, linear16[:, n % 2, :], ALU.add).then_inc(res_ready, 1)
                if live(i, j, L_PV):
                    n = j - L_PV
                    for u, m0 in row_units(n):
                        after(pool, probs_ready, tile_count(i, n))
                        after(pool, v_kept, tile_count(i, N * (n // N) + m0 + 3))
                        after(pool, pv_halved, unit_count(i, u - 2))
                        v = kv[:, 1, (n // N) % 2, m0:m0 + 4, :].rearrange("p m (h d) -> p (m h) d", d=D)
                        p = probs[:, n % 2, m0 * H:(m0 + 4) * H].unsqueeze(2).broadcast_to([P, 4 * H, D])
                        o = prod_pv[:, u % 2, :].rearrange("p (a d) -> p a d", d=D)
                        nc.gpsimd.tensor_tensor(o, v, p, ALU.mult).then_inc(pv_multiplied, 1)

            run_slots(pool, slot)

        @block.scalar
        def _(act):
            act.wait_ge(scales_ready, 1)
            for w in range(16):
                c, col = weight_place(w)
                dst = (wqkv_hi if w < 12 else wproj_hi)[:, c, col:col + 512]
                which = 0 if w < 12 else 1
                act.wait_ge(w_transposed, w + 1)
                nc.scalar.activation(dst, weight_bank(w)[:, :], ACT.Copy,
                                     scale=scale[:, which:which + 1]).then_inc(w_hi_ready, 1)

            def slot(i, j):
                if live(i, j, L_SOFT):
                    n = j - L_SOFT
                    keys = PROMPT if n % N < PROMPT else N
                    after(act, shifted_ready, tile_count(i, n))
                    after(act, probs_ready, tile_count(i, n - 1))
                    nc.scalar.activation(exps[:, 0:keys * H], shifted[:, 0:keys * H], ACT.Exp,
                                         scale=exp_scale[:, 0:1]).then_inc(exps_ready, 1)
                if live(i, j, L_TRANS):
                    n = j - L_TRANS
                    after(act, xT_ready, tile_count(i, n))
                    after(act, lin_summed, tile_count(i, n - 2))
                    nc.scalar.activation(xT_hi[:, n % 2, :], xT_ps[:, :], ACT.Copy)
                    nc.scalar.activation(xT_q[:, n % 2, :], xT_ps[:, :], ACT.Copy,
                                         saturate=False).then_inc(x_hi_q_ready, 1)
                if live(i, j, L_PROJ):
                    n = j - L_PROJ
                    after(act, oT_ready, tile_count(i, n))
                    after(act, proj_summed, tile_count(i, n - 1))
                    nc.scalar.activation(oT_hi[:, :], oT_ps[:, :], ACT.Copy).then_inc(o_hi_ready, 1)
                if live(i, j, L_QKV):
                    n = j - L_QKV
                    after(act, q_summed, tile_count(i, n))
                    after(act, qk_multiplied, unit_count(i, units_before(n - N + 1) - 1))
                    nc.scalar.activation(q[:, n % N, :], q_ps[:, :], ACT.Copy).then_inc(q_kept, 1)
                    g = n // N
                    after(act, k_summed, tile_count(i, n))
                    after(act, qk_multiplied, unit_count(i, UNITS * (g - 1) - 1))
                    nc.scalar.activation(kv[:, 0, g % 2, n % N, :], k_ps[:, :], ACT.Copy).then_inc(k_kept, 1)
                    after(act, v_summed, tile_count(i, n))
                    after(act, pv_multiplied, unit_count(i, UNITS * (g - 1) - 1))
                    nc.scalar.activation(kv[:, 1, g % 2, n % N, :], v_ps[:, :], ACT.Copy).then_inc(v_kept, 1)
                    after(act, lin_summed, tile_count(i, n))
                    after(act, res_ready, tile_count(i, n - 2))
                    nc.scalar.activation(linear16[:, n % 2, :], lin_ps[:, :], ACT.Copy).then_inc(lin_rounded, 1)

            run_slots(act, slot)

        @block.tensor
        def _(pe):
            pe.wait_ge(ident_ready, 1)
            for w in range(N_BANKS):
                c, col = weight_place(w)
                if w == 0:
                    pe.wait_ge(wqkv_loaded, 16)
                if w == 12:
                    pe.wait_ge(wproj_loaded, 16)
                if w == 16:
                    pe.wait_ge(wffn_quantised, 1)
                after(pe, w_ready, w - 1)
                for o in range(4):
                    if w < 12:
                        src = wqkv_nat[:, col // P + o, c * P:(c + 1) * P]
                    elif w < 16:
                        src = wproj_nat[:, o, c * P:(c + 1) * P]
                    else:
                        src = wffn_nat[:, o * C + c * P:o * C + (c + 1) * P]
                    last = nc.tensor.transpose(weight_bank(w)[:, o * P:(o + 1) * P], src, ident[:, :])
                last.then_inc(w_transposed, 1)
            pe.wait_ge(w_ready, N_BANKS)
            pe.wait_ge(consts_set, 4)
            pe.wait_ge(bias_moved, 32)

            def split_products(acc, t_hi, t_lo, w_hi, w_lo, col, first=True):
                parts = [(t, w, c) for c in range(KC) for t, w in ((t_hi, w_hi), (t_hi, w_lo))]
                parts += [(t_lo, w_hi, c) for c in range(KC)]
                for k, (t, w, c) in enumerate(parts):
                    last = nc.tensor.matmul(acc[:, :], t[:, c * P:(c + 1) * P], w[:, c, col:col + 512],
                                            start=first and k == 0, stop=k == len(parts) - 1)
                return last

            def slot(i, j):
                if live(i, j, L_TRANS):
                    n = j - L_TRANS
                    after(pe, xn_ready, tile_count(i, n))
                    after(pe, x_lo_ready, tile_count(i, n - 1))
                    for c in range(KC):
                        last = nc.tensor.transpose(xT_ps[:, c * P:(c + 1) * P], xn[:, c * P:(c + 1) * P],
                                                   ident[:, :])
                    last.then_inc(xT_ready, 1)
                if live(i, j, L_PROJ):
                    n = j - L_PROJ
                    parts = [(u, h) for u, _ in row_units(n) for h in range(2)]
                    after(pe, pv_halved, unit_count(i, parts[-1][0]))
                    after(pe, o_lo_ready, tile_count(i, n - 1))
                    for c in range(KC):
                        for k, (u, h) in enumerate(parts):
                            last = nc.tensor.matmul(
                                oT_ps[:, c * P:(c + 1) * P], halves[:, u % 4, h * C + c * P:h * C + (c + 1) * P],
                                ident[:, :], start=k == 0, stop=k == len(parts) - 1, is_transpose=True)
                    last.then_inc(oT_ready, 1)
                if live(i, j, L_QKV):
                    n = j - L_QKV
                    t_hi, t_lo, t_q = xT_hi[:, n % 2, :], xT_lo[:, n % 2, :], xT_q[:, n % 2, :]
                    after(pe, x_lo_ready, tile_count(i, n))
                    for k, (acc, kept, summed) in enumerate((
                            (q_ps, q_kept, q_summed), (k_ps, k_kept, k_summed), (v_ps, v_kept, v_summed))):
                        after(pe, kept, tile_count(i, n - 1))
                        if acc is v_ps:
                            after(pe, lin_rounded, tile_count(i, n - 1))
                        nc.tensor.matmul(acc[:, :], ones[:, :], bias_rows[:, k * C:(k + 1) * C],
                                         start=True, stop=False)
                        split_products(acc, t_hi, t_lo, wqkv_hi, wqkv_lo, k * C, first=False).then_inc(summed, 1)
                    for c in range(KC):
                        last = nc.tensor.matmul(lin_ps[:, :], t_q[:, c * P:(c + 1) * P], wffn_q[:, c, :],
                                                start=c == 0, stop=c == KC - 1)
                    last.then_inc(lin_summed, 1)
                if live(i, j, L_PROJ):
                    n = j - L_PROJ
                    after(pe, o_lo_ready, tile_count(i, n))
                    after(pe, y_ready, tile_count(i, n - 1))
                    split_products(proj_ps, oT_hi, oT_lo, wproj_hi, wproj_lo, 0).then_inc(proj_summed, 1)

            run_slots(pe, slot)

        @block.vector
        def _(dve):
            dve.wait_ge(wqkv_loaded, 16)
            nc.vector.tensor_reduce(amax[:, 0:1], wqkv_nat.rearrange("p j c -> p (j c)"), AX_X, ALU.max,
                                    apply_absolute_value=True).then_inc(amax_steps, 1)
            dve.wait_ge(bqkv_loaded, 16)
            nc.vector.tensor_reduce(amax[:, 2:3], bqkv_nat, AX_X, ALU.max,
                                    apply_absolute_value=True).then_inc(amax_steps, 1)
            dve.wait_ge(wproj_loaded, 16)
            nc.vector.tensor_reduce(amax[:, 1:2], wproj_nat.rearrange("p j c -> p (j c)"), AX_X, ALU.max,
                                    apply_absolute_value=True).then_inc(amax_steps, 1)
            dve.wait_ge(amax_steps, 3)
            nc.vector.scalar_tensor_tensor(out=amax[:, 0:1], in0=amax[:, 2:3], scalar=1.0 / 256,
                                           in1=amax[:, 0:1], op0=ALU.mult, op1=ALU.max).then_inc(amax_parts, 1)
            dve.wait_ge(amax_ready, 1)
            nc.vector.tensor_scalar(amax[:, 2:4], amax[:, 2:4], 2.0 ** -100, None, ALU.max).then_inc(scale_steps, 1)
            dve.wait_ge(scale_steps, 1)
            nc.vector.tensor_scalar(exponent[:, :], amax[:, 2:4].bitcast(I32), 0x7F800000, None,
                                    ALU.bitwise_and).then_inc(scale_steps, 1)
            dve.wait_ge(scale_steps, 2)
            nc.vector.tensor_scalar(scale[:, :].bitcast(I32), exponent[:, :], -1.0, 259.0 * 2 ** 23,
                                    ALU.mult, ALU.add).then_inc(scale_steps, 1)
            nc.vector.tensor_scalar(unscale[:, :].bitcast(I32), exponent[:, :], 5.0 * 2 ** 23, None,
                                    ALU.subtract).then_inc(scale_steps, 1)
            dve.wait_ge(scale_steps, 4)
            nc.vector.tensor_tensor(out_scale[:, :], unscale[:, 0:1], unscale[:, 1:2], ALU.mult).then_inc(scale_steps, 1)
            nc.vector.scalar_tensor_tensor(out=exp_scale[:, :], in0=unscale[:, 0:1], scalar=float(D) ** -0.5,
                                           in1=unscale[:, 0:1], op0=ALU.mult, op1=ALU.mult).then_inc(scales_ready, 1)
            dve.wait_ge(wffn_loaded, 16)
            nc.vector.tensor_scalar(is_large, wffn_nat, CHIP_FP8_MAX, -CHIP_FP8_MAX, ALU.min, ALU.max).then_inc(quant_steps, 1)
            nc.vector.tensor_scalar(half_w, wffn_nat, FP8_MAX, -FP8_MAX, ALU.min, ALU.max).then_inc(quant_steps, 1)
            dve.wait_ge(quant_steps, 2)
            nc.vector.tensor_copy(q_small, is_large, saturate=False).then_inc(quant_steps, 1)
            nc.vector.tensor_scalar(q_large, half_w, 0.5, None, ALU.mult, saturate=False).then_inc(quant_steps, 1)
            dve.wait_ge(quant_steps, 4)
            nc.vector.tensor_scalar(is_large, wffn_nat, 200.0, None, ALU.is_gt).then_inc(quant_steps, 1)
            nc.vector.scalar_tensor_tensor(out=half_w, in0=q_large, scalar=2.0, in1=q_small,
                                           op0=ALU.mult, op1=ALU.subtract).then_inc(quant_steps, 1)
            dve.wait_ge(quant_steps, 6)
            nc.vector.scalar_tensor_tensor(out=is_large, in0=wffn_nat, scalar=-200.0, in1=is_large,
                                           op0=ALU.is_lt, op1=ALU.add).then_inc(quant_steps, 1)
            dve.wait_ge(quant_steps, 7)
            nc.vector.tensor_tensor(half_w, half_w, is_large, ALU.mult).then_inc(quant_steps, 1)
            dve.wait_ge(quant_steps, 8)
            nc.vector.tensor_tensor(wffn_nat, half_w, q_small, ALU.add).then_inc(wffn_quantised, 1)
            for w in range(N_BANKS):
                c, col = weight_place(w)
                if w < 16:
                    which = 0 if w < 12 else 1
                    hi, lo = (wqkv_hi, wqkv_lo) if w < 12 else (wproj_hi, wproj_lo)
                    dve.wait_ge(w_hi_ready, w + 1)
                    nc.vector.scalar_tensor_tensor(out=lo[:, c, col:col + 512], in0=weight_bank(w)[:, :],
                                                   scalar=scale[:, which:which + 1], in1=hi[:, c, col:col + 512],
                                                   op0=ALU.mult, op1=ALU.subtract).then_inc(w_ready, 1)
                else:
                    dve.wait_ge(w_transposed, w + 1)
                    nc.vector.tensor_copy(wffn_q[:, c, :], weight_bank(w)[:, :]).then_inc(w_ready, 1)

            def slot(i, j):
                if live(i, j, L_SUM):
                    n = j - L_SUM
                    for u, _ in row_units(n):
                        after(dve, pv_multiplied, unit_count(i, u))
                        m = n - 4 if n % N < PROMPT else n - 2
                        after(dve, oT_ready, tile_count(i, m))
                        nc.vector.tensor_tensor(halves[:, u % 4, :], prod_pv[:, u % 2, 0:QUAD // 2],
                                                prod_pv[:, u % 2, QUAD // 2:QUAD], ALU.add).then_inc(pv_halved, 1)
                if live(i, j, L_SOFT):
                    n = j - L_SOFT
                    keys = PROMPT if n % N < PROMPT else N
                    e = exps[:, 0:keys * H].rearrange("p (m h) -> p m h", h=H)
                    after(dve, exps_ready, tile_count(i, n))
                    nc.vector.tensor_reduce(row_sum[:, :], e.rearrange("p m h -> p h m"), AX_X,
                                            ALU.add).then_inc(sum_steps, 1)
                if live(i, j, L_STATS):
                    n = j - L_STATS
                    r = n % 2
                    after(dve, x_loaded[n % PAIR], i * 16 + 16 * (n // PAIR + 1))
                    after(dve, xn_ready, tile_count(i, n - 2))
                    nc.vector.bn_stats(stats[:, r, :], xs[:, n % PAIR, :]).then_inc(stat_steps, 1)
                    after(dve, stat_steps, i * (2 * PAIR) + (2 * n + 1))
                if live(i, j, L_SOFT):
                    n = j - L_SOFT
                    after(dve, sum_steps, i * (2 * PAIR) + (2 * n + 1))
                    nc.vector.reciprocal(inv_sum[:, :], row_sum[:, :]).then_inc(sum_steps, 1)
                if live(i, j, L_STATS):
                    n = j - L_STATS
                    r = n % 2
                    nc.vector.bn_aggr(mean_var[:, r, :], stats[:, r, :]).then_inc(stat_steps, 1)
                if live(i, j, L_SOFT):
                    n = j - L_SOFT
                    after(dve, sum_steps, i * (2 * PAIR) + (2 * n + 2))
                    after(dve, pv_multiplied, unit_count(i, units_before(n - 1) - 1))
                    nc.vector.tensor_tensor(probs[:, n % 2, 0:keys * H].rearrange("p (m h) -> p m h", h=H), e,
                                            inv_sum[:, :].unsqueeze(1).broadcast_to([P, keys, H]),
                                            ALU.mult).then_inc(probs_ready, 1)
                if live(i, j, L_STATS):
                    n = j - L_STATS
                    r = n % 2
                    after(dve, stat_steps, i * (2 * PAIR) + (2 * n + 2))
                    after(dve, rstd_ready, tile_count(i, n - 2))
                    nc.vector.tensor_scalar(var_eps[:, r:r + 1], mean_var[:, r, 1:2], EPS, None,
                                            ALU.add).then_inc(var_ready, 1)
                if live(i, j, L_TRANS):
                    n = j - L_TRANS
                    after(dve, x_hi_q_ready, tile_count(i, n))
                    nc.vector.tensor_tensor(xT_lo[:, n % 2, :], xT_ps[:, :], xT_hi[:, n % 2, :],
                                            ALU.subtract).then_inc(x_lo_ready, 1)
                if live(i, j, L_OUT):
                    n = j - L_OUT
                    xt = xs[:, n % PAIR, :]
                    after(dve, proj_summed, tile_count(i, n))
                    after(dve, res_ready, tile_count(i, n))
                    nc.vector.scalar_tensor_tensor(out=xt, in0=proj_ps[:, :], scalar=out_scale[:, 0:1], in1=xt,
                                                   op0=ALU.mult, op1=ALU.add).then_inc(y_ready, 1)
                if live(i, j, L_PROJ):
                    n = j - L_PROJ
                    after(dve, o_hi_ready, tile_count(i, n))
                    after(dve, proj_summed, tile_count(i, n - 1))
                    nc.vector.tensor_tensor(oT_lo[:, :], oT_ps[:, :], oT_hi[:, :],
                                            ALU.subtract).then_inc(o_lo_ready, 1)
                if live(i, j, L_QK):
                    n = j - L_QK
                    keys = PROMPT if n % N < PROMPT else N
                    for u, m0 in row_units(n):
                        after(dve, q_kept, tile_count(i, n))
                        after(dve, k_kept, tile_count(i, N * (n // N) + m0 + 3))
                        after(dve, qk_reduced, unit_count(i, u - 1))
                        k = kv[:, 0, (n // N) % 2, m0:m0 + 4, :]
                        qb = q[:, n % N, :].unsqueeze(1).broadcast_to([P, 4, C])
                        nc.vector.tensor_tensor(prod_qk[:, :].rearrange("p (m c) -> p m c", c=C), qb, k,
                                                ALU.mult).then_inc(qk_multiplied, 1)
                        after(dve, qk_multiplied, unit_count(i, u))
                        after(dve, shifted_ready, tile_count(i, n - 1))
                        nc.vector.tensor_reduce(scores[:, m0 * H:(m0 + 4) * H],
                                                prod_qk[:, :].rearrange("p (a d) -> p a d", d=D), AX_X,
                                                ALU.add).then_inc(qk_reduced, 1)
                    sc = scores[:, 0:keys * H].rearrange("p (m h) -> p m h", h=H)
                    after(dve, qk_reduced, unit_count(i, row_units(n)[-1][0]))
                    nc.vector.tensor_reduce(row_max[:, :], sc.rearrange("p m h -> p h m"), AX_X,
                                            ALU.max).then_inc(max_ready, 1)
                    after(dve, max_ready, tile_count(i, n))
                    after(dve, exps_ready, tile_count(i, n - 1))
                    nc.vector.tensor_tensor(shifted[:, 0:keys * H].rearrange("p (m h) -> p m h", h=H), sc,
                                            row_max[:, :].unsqueeze(1).broadcast_to([P, keys, H]),
                                            ALU.subtract).then_inc(shifted_ready, 1)
                if live(i, j, L_NORM):
                    n = j - L_NORM
                    r = n % 2
                    after(dve, rstd_ready, tile_count(i, n))
                    after(dve, xT_ready, tile_count(i, n - 1))
                    nc.vector.tensor_scalar(xn[:, :], xs[:, n % PAIR, :], mean_var[:, r, 0:1], rstd[:, r:r + 1],
                                            ALU.subtract, ALU.mult).then_inc(xn_ready, 1)

            run_slots(dve, slot)


_INS = ['L0_attn_x', 'L0_attn_Wqkv', 'L0_attn_bqkv', 'L0_attn_Wproj', 'L0_attn_bproj', 'L0_ffn_weight', 'L0_ffn_bias']


def kernel(**inputs):
    import numpy as np
    import concourse.bacc as bacc
    from concourse.bass_utils import run_bass_kernel_spmd

    nc = bacc.Bacc("TRN2", target_bir_lowering=False, num_devices=1)
    arrays, args = {}, []
    for name in _INS:
        a = np.ascontiguousarray(inputs[name])
        arrays[f"in_{name}"] = a
        args.append(nc.dram_tensor(f"in_{name}", a.shape, mybir.dt.from_np(a.dtype), kind="ExternalInput").ap())
    shape = inputs['L0_attn_x'].shape
    args.append(nc.dram_tensor("out", shape, F32, kind="ExternalOutput").ap())
    attention_and_fp8_linear(nc, *args)
    r = run_bass_kernel_spmd(nc, [arrays], core_ids=[0])
    return r.results[0]["out"]
```

```python
from contextlib import ExitStack

import concourse.bass as bass
from concourse import mybir

F32 = mybir.dt.float32
F16 = mybir.dt.float16
BF16 = mybir.dt.bfloat16
FP8 = mybir.dt.float8e4
I32 = mybir.dt.int32
ALU = mybir.AluOpType
ACT = mybir.ActivationFunctionType
AX_X = mybir.AxisListType.X

P = 128
N = 8
B = 2048
C = 512
H = 16
D = C // H
KC = C // P
QKV = 3 * C
EPS = 1e-5
PROMPT = 4
TILES = N * B // P
PAIR = 2 * N
QUAD = 4 * C
UNITS = 12
FP8_MAX = 448.0
CHIP_FP8_MAX = 240.0

L_STATS, L_NORM, L_TRANS, L_KV, L_RES, L_Q, L_QK, L_SOFT, L_PV, L_SUM, L_PROJ, L_OUT, L_STORE = \
    2, 3, 4, 5, 6, 8, 9, 10, 12, 13, 14, 15, 15


def units_before(n):
    g, r = n // N, n % N
    return UNITS * g + r + max(0, r - 4)


def row_units(n):
    return [(units_before(n) + q, 4 * q) for q in range(1 if n % N < PROMPT else 2)]


def tile_count(i, n):
    return i * PAIR + (n + 1)


def unit_count(i, u):
    return i * (2 * UNITS) + (u + 1)


def after(eng, sem, count):
    if not isinstance(count, int) or count > 0:
        eng.wait_ge(sem, count)


def live(i, j, lag):
    return not isinstance(i, int) or 0 <= i * PAIR + j - lag < TILES


def run_slots(eng, slot):
    for j in range(PAIR):
        slot(0, j)
    with eng.Fori(1, TILES // PAIR) as i:
        for j in range(PAIR):
            slot(i, j)
    for j in range(PAIR):
        slot(TILES // PAIR, j)


def attention_and_fp8_linear(nc, x, Wqkv, bqkv, Wproj, bproj, Wffn, bffn, out):
    x_v = x.rearrange("n (i two b) c -> n i two b c", two=2, b=P)
    out_v = out.rearrange("n (i two b) c -> n i two b c", two=2, b=P)

    with ExitStack() as ctx:
        def sb(name, shape, dt):
            return ctx.enter_context(nc.sbuf_tensor(name, shape, dt))

        def bank(name):
            return ctx.enter_context(nc.psum_tensor(name, [P, 512], F32))

        def sem(name):
            return ctx.enter_context(nc.semaphore(name))

        wqkv_hi = sb("wqkv_hi", [P, KC, QKV], F16)
        wqkv_lo = sb("wqkv_lo", [P, KC, QKV], F16)
        wproj_hi = sb("wproj_hi", [P, KC, C], F16)
        wproj_lo = sb("wproj_lo", [P, KC, C], F16)
        wffn_q = sb("wffn_q", [P, KC, C], BF16)
        bias_rows = sb("bias_rows", [P, C], BF16)
        k_bias = sb("k_bias", [P, C], F32)
        v_bias_col = sb("v_bias_col", [P, KC], F32)
        ones = sb("ones", [P, P], BF16)
        ident = sb("ident", [P, P], F32)
        out_bias = sb("out_bias", [P, C], F32)
        amax = sb("amax", [P, 8], F32)
        scale = sb("scale", [P, 2], F32)
        unscale = sb("unscale", [P, 2], F32)
        exponent = sb("exponent", [P, 2], I32)
        exp_scale = sb("exp_scale", [P, 1], F32)
        out_scale = sb("out_scale", [P, 1], F32)
        minus_half = sb("minus_half", [P, 1], F32)

        xs = sb("xs", [P, PAIR, C], F32)
        stats = sb("stats", [P, 6], F32)
        mean_var = sb("mean_var", [P, 2, 2], F32)
        minus_mean = sb("minus_mean", [P, 1], F32)
        var_eps = sb("var_eps", [P, 1], F32)
        rstd = sb("rstd", [P, 1], F32)
        xn = sb("xn", [P, C], F32)
        xT_hi = sb("xT_hi", [P, N, C], F16)
        xT_lo = sb("xT_lo", [P, N, C], F16)
        xT_q = sb("xT_q", [P, 2, C], FP8)
        kv = sb("kv", [P, 2, 2, N, C], F32)
        linear16 = sb("linear16", [P, 2, C], F16)
        prod_qk = sb("prod_qk", [P, QUAD], F32)
        scores = sb("scores", [P, N * H], F32)
        row_max = sb("row_max", [P, H], F32)
        shifted = sb("shifted", [P, N * H], F32)
        exps = sb("exps", [P, N * H], F32)
        row_sum = sb("row_sum", [P, H], F32)
        inv_sum = sb("inv_sum", [P, H], F32)
        probs = sb("probs", [P, 4, N * H], F32)
        prod_pv = sb("prod_pv", [P, 2, QUAD], F32)
        halves = sb("halves", [P, 4, QUAD // 2], F32)
        oT_hi = sb("oT_hi", [P, C], F16)
        oT_lo = sb("oT_lo", [P, C], F16)
        projected = sb("projected", [P, C], F32)

        xT_ps, oT_ps, k_ps, v_ps, lin_ps, proj_ps = (
            bank(n) for n in ("xT_ps", "oT_ps", "k_ps", "v_ps", "lin_ps", "proj_ps"))
        q_ps = (bank("q_ps0"), bank("q_ps1"))

        scratch = kv[:, :, :, :, :].rearrange("p a b m c -> p (a b m c)")
        wqkv_nat = scratch[:, 0:6144].rearrange("p (j c) -> p j c", c=C)
        wproj_nat = scratch[:, 6144:8192].rearrange("p (j c) -> p j c", c=C)
        wffn_nat = scratch[:, 8192:10240]
        clipped = scratch[:, 10240:12288]
        half_w = scratch[:, 12288:14336]
        q_small = scratch[:, 14336:14848].bitcast(FP8)
        q_half_small = scratch[:, 14848:15360].bitcast(FP8)
        q_half = scratch[:, 15360:15872].bitcast(FP8)
        diagonals = scratch[:, 15872:16064].bitcast(BF16).rearrange("p (a n) -> p a n", n=P)
        bqkv_nat = halves[:, 3, 0:QKV // P]
        bias_row = prod_pv[0:1, 0, 0:C]
        bias_rest = prod_pv[0:1, 1, 0:C]
        bias_mid = halves[0:1, 0, 0:C // 2].bitcast(BF16)
        bias_low = halves[0:1, 1, 0:C // 2].bitcast(BF16)
        bffn_all = halves[:, 2, 0:C]

        wk_loaded = sem("wk_loaded")
        wv_loaded = sem("wv_loaded")
        wq_loaded = sem("wq_loaded")
        wproj_loaded = sem("wproj_loaded")
        wffn_loaded = sem("wffn_loaded")
        bqkv_loaded = sem("bqkv_loaded")
        biases_loaded = sem("biases_loaded")
        bias_row_loaded = sem("bias_row_loaded")
        consts_set = sem("consts_set")
        ident_ready = sem("ident_ready")
        amax_steps = sem("amax_steps")
        amax_parts = sem("amax_parts")
        amax_ready = sem("amax_ready")
        scale_steps = sem("scale_steps")
        scales_ready = sem("scales_ready")
        bias_steps = sem("bias_steps")
        bias_split = sem("bias_split")
        bias_moved = sem("bias_moved")
        k_bias_loaded = sem("k_bias_loaded")
        k_bias_ready = sem("k_bias_ready")
        v_bias_loaded = sem("v_bias_loaded")
        v_bias_split = sem("v_bias_split")
        v_bias_projected = sem("v_bias_projected")
        biases_added = sem("biases_added")
        out_bias_ready = sem("out_bias_ready")
        wffn_clipped = sem("wffn_clipped")
        wffn_halved = sem("wffn_halved")
        q_half_ready = sem("q_half_ready")
        small_ready = sem("small_ready")
        diagonals_ready = sem("diagonals_ready")
        wffn_transposed = sem("wffn_transposed")
        wffn_ready = sem("wffn_ready")
        w_transposed = sem("w_transposed")
        w_hi_ready = sem("w_hi_ready")
        w_ready = sem("w_ready")

        x_loaded = [sem(f"x_loaded{k}") for k in range(PAIR)]
        y_stored = [sem(f"y_stored{k}") for k in range(PAIR)]
        stats_ready = sem("stats_ready")
        mean_var_ready = sem("mean_var_ready")
        minus_mean_ready = sem("minus_mean_ready")
        centred_ready = sem("centred_ready")
        var_ready = sem("var_ready")
        rstd_ready = sem("rstd_ready")
        xn_ready = sem("xn_ready")
        xT_ready = sem("xT_ready")
        x_hi_q_ready = sem("x_hi_q_ready")
        x_lo_ready = sem("x_lo_ready")
        q_summed, k_summed, v_summed, lin_summed = (
            sem(n) for n in ("q_summed", "k_summed", "v_summed", "lin_summed"))
        k_copied, k_kept, v_kept, lin_rounded = (
            sem(n) for n in ("k_copied", "k_kept", "v_kept", "lin_rounded"))
        res_step = sem("res_step")
        res_ready = sem("res_ready")
        qk_multiplied = sem("qk_multiplied")
        qk_reduced = sem("qk_reduced")
        max_ready = sem("max_ready")
        shifted_ready = sem("shifted_ready")
        exps_ready = sem("exps_ready")
        sum_steps = sem("sum_steps")
        probs_ready = sem("probs_ready")
        pv_multiplied = sem("pv_multiplied")
        pv_halved = sem("pv_halved")
        pv_summed = sem("pv_summed")
        oT_ready = sem("oT_ready")
        o_hi_ready = sem("o_hi_ready")
        o_lo_ready = sem("o_lo_ready")
        proj_summed = sem("proj_summed")
        proj_scaled = sem("proj_scaled")
        y_ready = sem("y_ready")

        banks = (lin_ps, proj_ps, k_ps, v_ps, xT_ps, oT_ps, *q_ps)
        N_PARTS = 4 * KC

        def part_bank(w):
            return banks[(KC + w) % len(banks)]

        def part_place(w):
            what, c = w // KC, w % KC
            if what == 3:
                return wproj_hi, wproj_lo, c, 0, 1
            return wqkv_hi, wqkv_lo, c, (C, 2 * C, 0)[what], 0

        block = ctx.enter_context(nc.Block())

        @block.sync
        def _(sp):
            sp.dma_start(wffn_nat.rearrange("p (j c) -> p j c", c=C),
                         Wffn.rearrange("(j p) c -> p j c", p=P)).then_inc(wffn_loaded, 16)
            Wqkv_v = Wqkv.rearrange("(j p) c -> p j c", p=P)
            sp.dma_start(wqkv_nat[:, KC:2 * KC], Wqkv_v[:, KC:2 * KC]).then_inc(wk_loaded, 16)
            sp.dma_start(wqkv_nat[:, 2 * KC:3 * KC], Wqkv_v[:, 2 * KC:3 * KC]).then_inc(wv_loaded, 16)
            sp.dma_start(wqkv_nat[:, 0:KC], Wqkv_v[:, 0:KC]).then_inc(wq_loaded, 16)
            sp.dma_start(wproj_nat, Wproj.rearrange("(j p) c -> p j c", p=P)).then_inc(wproj_loaded, 16)
            sp.dma_start(bqkv_nat, bqkv.rearrange("(p j) -> p j", p=P)).then_inc(bqkv_loaded, 16)
            sp.dma_start(bias_row, bqkv[0:C].rearrange("(a n) -> a n", a=1)).then_inc(bias_row_loaded, 16)
            sp.dma_start(k_bias[:, :], bqkv[C:2 * C].partition_broadcast(P)).then_inc(k_bias_loaded, 16)
            with nc.allow_non_contiguous_dma(reason="512 numbers, once"):
                sp.dma_start(v_bias_col[:, :], bqkv[2 * C:3 * C].rearrange("(k p) -> p k", p=P)).then_inc(v_bias_loaded, 16)
            sp.dma_start(out_bias[:, :], bproj.partition_broadcast(P)).then_inc(biases_loaded, 16)
            sp.dma_start(bffn_all, bffn.partition_broadcast(P)).then_inc(biases_loaded, 16)

            def slot(i, j):
                if isinstance(i, int) and (i, j) == (0, 4):
                    sp.wait_ge(bias_split, 1)
                    sp.dma_start(bias_rows[1:2, :], bias_mid).then_inc(bias_moved, 16)
                    sp.dma_start(bias_rows[2:3, :], bias_low).then_inc(bias_moved, 16)
                if live(i, j, 0):
                    after(sp, y_stored[j], i * 16)
                    sp.dma_start(xs[:, j, :], x_v[j % N, i, j // N]).then_inc(x_loaded[j], 16)
                if live(i, j, L_STORE):
                    n = j - L_STORE
                    after(sp, y_ready, tile_count(i, n))
                    sp.dma_start(out_v[n % N, i + n // PAIR, (n // N) % 2],
                                 xs[:, n % PAIR, :]).then_inc(y_stored[n % PAIR], 16)

            run_slots(sp, slot)
            for k in range(PAIR):
                sp.wait_ge(y_stored[k], 16 * (TILES // PAIR))

        @block.gpsimd
        def _(pool):
            nc.gpsimd.memset(ident[:, :], 0.0).then_inc(consts_set, 1)
            pool.wait_ge(consts_set, 1)
            nc.gpsimd.affine_select(out=ident[:, :], in_=ident[:, :], compare_op=ALU.not_equal, fill=1.0,
                                    base=0, pattern=[[-1, P]], channel_multiplier=1).then_inc(ident_ready, 1)
            nc.gpsimd.memset(ones[:, :], 1.0).then_inc(consts_set, 1)
            nc.gpsimd.memset(minus_half[:, :], -0.5).then_inc(consts_set, 1)
            nc.gpsimd.memset(bias_rows[:, :], 0.0).then_inc(consts_set, 1)
            pool.wait_ge(biases_loaded, 32)
            nc.gpsimd.tensor_tensor(out_bias[:, :], out_bias[:, :], bffn_all, ALU.add).then_inc(biases_added, 1)
            pool.wait_ge(amax_parts, 1)
            nc.gpsimd.partition_all_reduce(amax[:, 6:8], amax[:, 4:6], P,
                                           bass.bass_isa.ReduceOp.max).then_inc(amax_ready, 1)
            pool.wait_ge(scales_ready, 1)
            pool.wait_ge(k_bias_loaded, 16)
            nc.gpsimd.tensor_scalar(k_bias[:, :], k_bias[:, :], scale[:, 0:1], 1.0, ALU.mult, ALU.mult).then_inc(k_bias_ready, 1)
            pool.wait_ge(bias_row_loaded, 16)
            pool.wait_ge(consts_set, 4)
            nc.gpsimd.tensor_scalar(bias_row, bias_row, scale[0:1, 0:1], 1.0, ALU.mult, ALU.mult).then_inc(bias_steps, 1)
            pool.wait_ge(bias_steps, 1)
            nc.gpsimd.tensor_copy(bias_rows[0:1, :], bias_row).then_inc(bias_steps, 1)
            pool.wait_ge(bias_steps, 2)
            nc.gpsimd.tensor_tensor(bias_rest, bias_row, bias_rows[0:1, :], ALU.subtract).then_inc(bias_steps, 1)
            pool.wait_ge(bias_steps, 3)
            nc.gpsimd.tensor_copy(bias_mid, bias_rest).then_inc(bias_steps, 1)
            pool.wait_ge(bias_steps, 4)
            nc.gpsimd.tensor_tensor(bias_rest, bias_rest, bias_mid, ALU.subtract).then_inc(bias_steps, 1)
            pool.wait_ge(bias_steps, 5)
            nc.gpsimd.tensor_copy(bias_low, bias_rest).then_inc(bias_split, 1)

            def slot(i, j):
                if live(i, j, L_RES):
                    n = j - L_RES
                    xt = xs[:, n % PAIR, :]
                    if isinstance(i, int) and (i, n) == (0, 0):
                        pool.wait_ge(out_bias_ready, 1)
                    after(pool, centred_ready, tile_count(i, n))
                    nc.gpsimd.tensor_tensor(xt, xt, out_bias[:, :], ALU.add).then_inc(res_step, 1)
                    after(pool, res_step, tile_count(i, n))
                    after(pool, lin_rounded, tile_count(i, n))
                    nc.gpsimd.tensor_tensor(xt, xt, linear16[:, n % 2, :], ALU.add).then_inc(res_ready, 1)
                if live(i, j, L_OUT):
                    n = j - L_OUT
                    xt = xs[:, n % PAIR, :]
                    after(pool, proj_scaled, tile_count(i, n))
                    after(pool, res_ready, tile_count(i, n))
                    nc.gpsimd.tensor_tensor(xt, xt, projected[:, :], ALU.add).then_inc(y_ready, 1)
                if live(i, j, L_NORM):
                    n = j - L_NORM
                    after(pool, var_ready, tile_count(i, n))
                    after(pool, xn_ready, tile_count(i, n - 1))
                    nc.gpsimd.tensor_tensor(rstd[:, :], var_eps[:, :], minus_half[:, :],
                                            ALU.pow).then_inc(rstd_ready, 1)
                if live(i, j, L_PV):
                    n = j - L_PV
                    for u, m0 in row_units(n):
                        after(pool, probs_ready, tile_count(i, n))
                        after(pool, v_kept, tile_count(i, N * (n // N) + m0 + 3))
                        after(pool, pv_halved, unit_count(i, u - 2))
                        v = kv[:, 1, (n // N) % 2, m0:m0 + 4, :].rearrange("p m (h d) -> p (m h) d", d=D)
                        p = probs[:, n % 4, m0 * H:(m0 + 4) * H].unsqueeze(2).broadcast_to([P, 4 * H, D])
                        o = prod_pv[:, u % 2, :].rearrange("p (a d) -> p a d", d=D)
                        nc.gpsimd.tensor_tensor(o, v, p, ALU.mult).then_inc(pv_multiplied, 1)
                if live(i, j, L_KV):
                    n = j - L_KV
                    k = kv[:, 0, (n // N) % 2, n % N, :]
                    if isinstance(i, int) and (i, n) == (0, 0):
                        pool.wait_ge(k_bias_ready, 1)
                    after(pool, k_copied, tile_count(i, n))
                    nc.gpsimd.tensor_tensor(k, k, k_bias[:, :], ALU.add).then_inc(k_kept, 1)

            run_slots(pool, slot)

        @block.scalar
        def _(act):
            act.wait_ge(ident_ready, 1)
            for a, factor in enumerate((1.0, 2.0, -2.0)):
                nc.scalar.activation(diagonals[:, a, :], ident[:, :], ACT.Copy, scale=factor).then_inc(diagonals_ready, 1)
            act.wait_ge(wffn_clipped, 1)
            nc.scalar.activation(q_small, clipped, ACT.Copy, saturate=False).then_inc(small_ready, 1)
            nc.scalar.activation(q_half_small, clipped, ACT.Copy, scale=0.5, saturate=False).then_inc(small_ready, 1)
            for c in range(KC):
                act.wait_ge(wffn_transposed, c + 1)
                nc.scalar.activation(wffn_q[:, c, :], banks[c][:, :], ACT.Copy).then_inc(wffn_ready, 1)
            act.wait_ge(scales_ready, 1)
            for w in range(N_PARTS):
                hi, _, c, col, which = part_place(w)
                act.wait_ge(w_transposed, w + 1)
                nc.scalar.activation(hi[:, c, col:col + 512], part_bank(w)[:, :], ACT.Copy,
                                     scale=scale[:, which:which + 1]).then_inc(w_hi_ready, 1)

            def slot(i, j):
                if live(i, j, L_TRANS):
                    n = j - L_TRANS
                    after(act, xT_ready, tile_count(i, n))
                    after(act, q_summed, tile_count(i, n - N))
                    after(act, lin_summed, tile_count(i, n - 2))
                    nc.scalar.activation(xT_hi[:, n % N, :], xT_ps[:, :], ACT.Copy)
                    nc.scalar.activation(xT_q[:, n % 2, :], xT_ps[:, :], ACT.Copy,
                                         saturate=False).then_inc(x_hi_q_ready, 1)
                if live(i, j, L_PROJ):
                    n = j - L_PROJ
                    after(act, oT_ready, tile_count(i, n))
                    after(act, proj_summed, tile_count(i, n - 1))
                    nc.scalar.activation(oT_hi[:, :], oT_ps[:, :], ACT.Copy).then_inc(o_hi_ready, 1)
                if live(i, j, L_OUT):
                    n = j - L_OUT
                    after(act, proj_summed, tile_count(i, n))
                    after(act, y_ready, tile_count(i, n - 1))
                    nc.scalar.activation(projected[:, :], proj_ps[:, :], ACT.Copy,
                                         scale=out_scale[:, 0:1]).then_inc(proj_scaled, 1)
                if live(i, j, L_NORM):
                    n = j - L_NORM
                    r = n % 2
                    after(act, mean_var_ready, tile_count(i, n))
                    after(act, rstd_ready, tile_count(i, n - 1))
                    nc.scalar.activation(var_eps[:, :], mean_var[:, r, 1:2], ACT.Copy, bias=EPS).then_inc(var_ready, 1)
                    after(act, centred_ready, tile_count(i, n - 1))
                    nc.scalar.activation(minus_mean[:, :], mean_var[:, r, 0:1], ACT.Copy,
                                         scale=-1.0).then_inc(minus_mean_ready, 1)
                if live(i, j, L_KV):
                    n = j - L_KV
                    g = n // N
                    after(act, k_summed, tile_count(i, n))
                    after(act, qk_multiplied, unit_count(i, UNITS * (g - 1) - 1))
                    nc.scalar.activation(kv[:, 0, g % 2, n % N, :], k_ps[:, :], ACT.Copy).then_inc(k_copied, 1)
                if live(i, j, L_NORM):
                    n = j - L_NORM
                    after(act, minus_mean_ready, tile_count(i, n))
                    after(act, xT_ready, tile_count(i, n - 1))
                    nc.scalar.activation(xn[:, :], xs[:, n % PAIR, :], ACT.Identity,
                                         bias=minus_mean[:, 0:1]).then_inc(centred_ready, 1)
                if live(i, j, L_KV):
                    after(act, v_summed, tile_count(i, n := j - L_KV))
                    after(act, pv_multiplied, unit_count(i, UNITS * (n // N - 1) - 1))
                    nc.scalar.activation(kv[:, 1, (n // N) % 2, n % N, :], v_ps[:, :], ACT.Copy).then_inc(v_kept, 1)
                if live(i, j, L_SOFT):
                    n = j - L_SOFT
                    keys = PROMPT if n % N < PROMPT else N
                    after(act, shifted_ready, tile_count(i, n))
                    after(act, probs_ready, tile_count(i, n - 1))
                    nc.scalar.activation(exps[:, 0:keys * H], shifted[:, 0:keys * H], ACT.Exp,
                                         scale=exp_scale[:, 0:1]).then_inc(exps_ready, 1)
                if live(i, j, L_NORM):
                    n = j - L_NORM
                    after(act, centred_ready, tile_count(i, n))
                    after(act, rstd_ready, tile_count(i, n))
                    nc.scalar.activation(xn[:, :], xn[:, :], ACT.Copy,
                                         scale=rstd[:, 0:1]).then_inc(xn_ready, 1)
                if live(i, j, L_KV):
                    n = j - L_KV
                    after(act, lin_summed, tile_count(i, n))
                    after(act, res_ready, tile_count(i, n - 2))
                    nc.scalar.activation(linear16[:, n % 2, :], lin_ps[:, :], ACT.Copy).then_inc(lin_rounded, 1)

            run_slots(act, slot)

        @block.tensor
        def _(pe):
            pe.wait_ge(ident_ready, 1)
            pe.wait_ge(diagonals_ready, 3)
            pe.wait_ge(small_ready, 2)
            pe.wait_ge(q_half_ready, 1)
            for c in range(KC):
                for o in range(KC):
                    src = slice(o * C + c * P, o * C + (c + 1) * P)
                    for a, part in enumerate((q_small, q_half, q_half_small)):
                        last = nc.tensor.matmul(banks[c][:, o * P:(o + 1) * P], part[:, src], diagonals[:, a, :],
                                                start=a == 0, stop=a == 2)
                last.then_inc(wffn_transposed, 1)
            for w in range(N_PARTS):
                _, _, c, col, which = part_place(w)
                if w % KC == 0:
                    pe.wait_ge((wk_loaded, wv_loaded, wq_loaded, wproj_loaded)[w // KC], 16)
                if len(banks) - KC <= w < len(banks):
                    pe.wait_ge(wffn_ready, w - (len(banks) - KC) + 1)
                if w >= len(banks):
                    pe.wait_ge(w_ready, w - len(banks) + 1)
                for o in range(4):
                    nat = wproj_nat[:, o, :] if which else wqkv_nat[:, col // P + o, :]
                    last = nc.tensor.transpose(part_bank(w)[:, o * P:(o + 1) * P], nat[:, c * P:(c + 1) * P],
                                               ident[:, :])
                last.then_inc(w_transposed, 1)
            pe.wait_ge(w_ready, N_PARTS)
            pe.wait_ge(consts_set, 4)
            pe.wait_ge(bias_moved, 32)

            def split_products(acc, t_hi, t_lo, w_hi, w_lo, col, first=True):
                parts = [(t, w, c) for c in range(KC) for t, w in ((t_hi, w_hi), (t_hi, w_lo))]
                parts += [(t_lo, w_hi, c) for c in range(KC)]
                for k, (t, w, c) in enumerate(parts):
                    last = nc.tensor.matmul(acc[:, :], t[:, c * P:(c + 1) * P], w[:, c, col:col + 512],
                                            start=first and k == 0, stop=k == len(parts) - 1)
                return last

            def slot(i, j):
                if isinstance(i, int) and (i, j) == (0, L_KV):
                    pe.wait_ge(v_bias_split, 1)
                    split_products(proj_ps, oT_hi, oT_lo, wproj_hi, wproj_lo, 0).then_inc(v_bias_projected, 1)
                if live(i, j, L_TRANS):
                    n = j - L_TRANS
                    after(pe, xn_ready, tile_count(i, n))
                    after(pe, x_lo_ready, tile_count(i, n - 1))
                    for c in range(KC):
                        last = nc.tensor.transpose(xT_ps[:, c * P:(c + 1) * P], xn[:, c * P:(c + 1) * P],
                                                   ident[:, :])
                    last.then_inc(xT_ready, 1)
                if live(i, j, L_PROJ):
                    n = j - L_PROJ
                    units = [u for u, _ in row_units(n)]
                    after(pe, pv_summed, unit_count(i, units[-1]))
                    after(pe, o_lo_ready, tile_count(i, n - 1))
                    for c in range(KC):
                        for k, u in enumerate(units):
                            last = nc.tensor.matmul(
                                oT_ps[:, c * P:(c + 1) * P], halves[:, u % 4, c * P:(c + 1) * P],
                                ident[:, :], start=k == 0, stop=k == len(units) - 1, is_transpose=True)
                    last.then_inc(oT_ready, 1)
                if live(i, j, L_KV):
                    n = j - L_KV
                    t_hi, t_lo = xT_hi[:, n % N, :], xT_lo[:, n % N, :]
                    after(pe, x_lo_ready, tile_count(i, n))
                    after(pe, k_copied, tile_count(i, n - 1))
                    split_products(k_ps, t_hi, t_lo, wqkv_hi, wqkv_lo, C).then_inc(k_summed, 1)
                    after(pe, v_kept, tile_count(i, n - 1))
                    after(pe, lin_rounded, tile_count(i, n - 1))
                    split_products(v_ps, t_hi, t_lo, wqkv_hi, wqkv_lo, 2 * C).then_inc(v_summed, 1)
                if live(i, j, L_Q):
                    n = j - L_Q
                    acc = q_ps[n % 2]
                    after(pe, qk_multiplied, unit_count(i, units_before(n - 1) - 1))
                    nc.tensor.matmul(acc[:, :], ones[:, :], bias_rows[:, :], start=True, stop=False)
                    split_products(acc, xT_hi[:, n % N, :], xT_lo[:, n % N, :], wqkv_hi, wqkv_lo, 0,
                                   first=False).then_inc(q_summed, 1)
                if live(i, j, L_KV):
                    n = j - L_KV
                    for c in range(KC):
                        last = nc.tensor.matmul(lin_ps[:, :], xT_q[:, n % 2, c * P:(c + 1) * P], wffn_q[:, c, :],
                                                start=c == 0, stop=c == KC - 1)
                    last.then_inc(lin_summed, 1)
                if live(i, j, L_PROJ):
                    n = j - L_PROJ
                    after(pe, o_lo_ready, tile_count(i, n))
                    after(pe, proj_scaled, tile_count(i, n - 1))
                    split_products(proj_ps, oT_hi, oT_lo, wproj_hi, wproj_lo, 0).then_inc(proj_summed, 1)

            run_slots(pe, slot)

        @block.vector
        def _(dve):
            dve.wait_ge(wffn_loaded, 16)
            nc.vector.tensor_scalar(clipped, wffn_nat, CHIP_FP8_MAX, -CHIP_FP8_MAX, ALU.min,
                                    ALU.max).then_inc(wffn_clipped, 1)
            nc.vector.tensor_scalar(half_w, wffn_nat, 0.5, FP8_MAX / 2, ALU.mult, ALU.min).then_inc(wffn_halved, 1)
            dve.wait_ge(wffn_halved, 1)
            nc.vector.tensor_scalar(q_half, half_w, -FP8_MAX / 2, None, ALU.max, saturate=False).then_inc(q_half_ready, 1)
            for a, (loaded, at) in enumerate(((wk_loaded, KC), (wv_loaded, 2 * KC), (wq_loaded, 0))):
                dve.wait_ge(loaded, 16)
                nc.vector.tensor_reduce(amax[:, a:a + 1], wqkv_nat[:, at:at + KC].rearrange("p j c -> p (j c)"),
                                        AX_X, ALU.max, apply_absolute_value=True).then_inc(amax_steps, 1)
            dve.wait_ge(wproj_loaded, 16)
            nc.vector.tensor_reduce(amax[:, 5:6], wproj_nat.rearrange("p j c -> p (j c)"), AX_X, ALU.max,
                                    apply_absolute_value=True).then_inc(amax_steps, 1)
            dve.wait_ge(bqkv_loaded, 16)
            nc.vector.tensor_reduce(amax[:, 3:4], bqkv_nat, AX_X, ALU.max,
                                    apply_absolute_value=True).then_inc(amax_steps, 1)
            dve.wait_ge(amax_steps, 3)
            nc.vector.tensor_reduce(amax[:, 4:5], amax[:, 0:3], AX_X, ALU.max).then_inc(amax_steps, 1)
            dve.wait_ge(amax_steps, 6)
            nc.vector.scalar_tensor_tensor(out=amax[:, 4:5], in0=amax[:, 3:4], scalar=1.0 / 256,
                                           in1=amax[:, 4:5], op0=ALU.mult, op1=ALU.max).then_inc(amax_parts, 1)
            dve.wait_ge(amax_ready, 1)
            nc.vector.tensor_scalar(amax[:, 6:8], amax[:, 6:8], 2.0 ** -100, None, ALU.max).then_inc(scale_steps, 1)
            dve.wait_ge(scale_steps, 1)
            nc.vector.tensor_scalar(exponent[:, :], amax[:, 6:8].bitcast(I32), 0x7F800000, None,
                                    ALU.bitwise_and).then_inc(scale_steps, 1)
            dve.wait_ge(scale_steps, 2)
            nc.vector.tensor_scalar(scale[:, :].bitcast(I32), exponent[:, :], -1.0, 259.0 * 2 ** 23,
                                    ALU.mult, ALU.add).then_inc(scale_steps, 1)
            nc.vector.tensor_scalar(unscale[:, :].bitcast(I32), exponent[:, :], 5.0 * 2 ** 23, None,
                                    ALU.subtract).then_inc(scale_steps, 1)
            dve.wait_ge(scale_steps, 4)
            nc.vector.tensor_tensor(out_scale[:, :], unscale[:, 0:1], unscale[:, 1:2], ALU.mult).then_inc(scale_steps, 1)
            nc.vector.scalar_tensor_tensor(out=exp_scale[:, :], in0=unscale[:, 0:1], scalar=float(D) ** -0.5,
                                           in1=unscale[:, 0:1], op0=ALU.mult, op1=ALU.mult).then_inc(scales_ready, 1)
            for w in range(N_PARTS):
                hi, lo, c, col, which = part_place(w)
                dve.wait_ge(w_hi_ready, w + 1)
                nc.vector.scalar_tensor_tensor(out=lo[:, c, col:col + 512], in0=part_bank(w)[:, :],
                                               scalar=scale[:, which:which + 1], in1=hi[:, c, col:col + 512],
                                               op0=ALU.mult, op1=ALU.subtract).then_inc(w_ready, 1)
            dve.wait_ge(v_bias_loaded, 16)
            v_bias = v_bias_col[:, :].unsqueeze(2).broadcast_to([P, KC, P])
            bias_hi = oT_hi[:, :].rearrange("p (k t) -> p k t", t=P)
            dve.wait_ge(scales_ready, 1)
            nc.vector.tensor_scalar(bias_hi, v_bias, scale[:, 0:1], None, ALU.mult).then_inc(scale_steps, 1)
            dve.wait_ge(scale_steps, 6)
            nc.vector.scalar_tensor_tensor(out=oT_lo[:, :].rearrange("p (k t) -> p k t", t=P), in0=v_bias,
                                           scalar=scale[:, 0:1], in1=bias_hi,
                                           op0=ALU.mult, op1=ALU.subtract).then_inc(v_bias_split, 1)

            def scores_of_unit(i, n, u, m0):
                after(dve, q_summed, tile_count(i, n))
                after(dve, k_kept, tile_count(i, N * (n // N) + m0 + 3))
                after(dve, qk_reduced, unit_count(i, u - 1))
                k = kv[:, 0, (n // N) % 2, m0:m0 + 4, :]
                qb = q_ps[n % 2][:, :].unsqueeze(1).broadcast_to([P, 4, C])
                nc.vector.tensor_tensor(prod_qk[:, :].rearrange("p (m c) -> p m c", c=C), qb, k,
                                        ALU.mult).then_inc(qk_multiplied, 1)
                after(dve, qk_multiplied, unit_count(i, u))
                after(dve, shifted_ready, tile_count(i, n - 1))
                nc.vector.tensor_reduce(scores[:, m0 * H:(m0 + 4) * H],
                                        prod_qk[:, :].rearrange("p (a d) -> p a d", d=D), AX_X,
                                        ALU.add).then_inc(qk_reduced, 1)

            def slot(i, j):
                if isinstance(i, int) and (i, j) == (0, L_RES):
                    dve.wait_ge(v_bias_projected, 1)
                    dve.wait_ge(biases_added, 1)
                    nc.vector.scalar_tensor_tensor(out=out_bias[:, :], in0=proj_ps[:, :], scalar=out_scale[:, 0:1],
                                                   in1=out_bias[:, :], op0=ALU.mult, op1=ALU.add).then_inc(out_bias_ready, 1)
                if live(i, j, L_TRANS):
                    n = j - L_TRANS
                    after(dve, x_hi_q_ready, tile_count(i, n))
                    nc.vector.tensor_tensor(xT_lo[:, n % N, :], xT_ps[:, :], xT_hi[:, n % N, :],
                                            ALU.subtract).then_inc(x_lo_ready, 1)
                if live(i, j, L_PROJ):
                    n = j - L_PROJ
                    after(dve, o_hi_ready, tile_count(i, n))
                    after(dve, proj_summed, tile_count(i, n - 1))
                    nc.vector.tensor_tensor(oT_lo[:, :], oT_ps[:, :], oT_hi[:, :],
                                            ALU.subtract).then_inc(o_lo_ready, 1)
                if live(i, j, L_SUM):
                    n = j - L_SUM
                    for u, _ in row_units(n):
                        after(dve, pv_multiplied, unit_count(i, u))
                        after(dve, oT_ready, tile_count(i, n - 4 if n % N < PROMPT else n - 2))
                        nc.vector.tensor_tensor(halves[:, u % 4, :], prod_pv[:, u % 2, 0:QUAD // 2],
                                                prod_pv[:, u % 2, QUAD // 2:QUAD], ALU.add).then_inc(pv_halved, 1)
                if live(i, j, L_STATS):
                    n = j - L_STATS
                    after(dve, x_loaded[n % PAIR], i * 16 + 16 * (n // PAIR + 1))
                    after(dve, mean_var_ready, tile_count(i, n - 1))
                    nc.vector.bn_stats(stats[:, :], xs[:, n % PAIR, :]).then_inc(stats_ready, 1)
                    after(dve, minus_mean_ready, tile_count(i, n - 2))
                    after(dve, stats_ready, tile_count(i, n))
                if live(i, j, L_SUM):
                    for u, _ in row_units(j - L_SUM):
                        after(dve, pv_halved, unit_count(i, u))
                        nc.vector.tensor_tensor(halves[:, u % 4, 0:C], halves[:, u % 4, 0:C],
                                                halves[:, u % 4, C:2 * C], ALU.add).then_inc(pv_summed, 1)
                if live(i, j, L_STATS):
                    n = j - L_STATS
                    nc.vector.bn_aggr(mean_var[:, n % 2, :], stats[:, :]).then_inc(mean_var_ready, 1)
                if live(i, j, L_QK):
                    n = j - L_QK
                    scores_of_unit(i, n, *row_units(n)[0])
                if live(i, j, L_SOFT):
                    n = j - L_SOFT
                    keys = PROMPT if n % N < PROMPT else N
                    e = exps[:, 0:keys * H].rearrange("p (m h) -> p m h", h=H)
                    after(dve, exps_ready, tile_count(i, n))
                    nc.vector.tensor_reduce(row_sum[:, :], e.rearrange("p m h -> p h m"), AX_X,
                                            ALU.add).then_inc(sum_steps, 1)
                    after(dve, sum_steps, i * (2 * PAIR) + (2 * n + 1))
                    nc.vector.reciprocal(inv_sum[:, :], row_sum[:, :]).then_inc(sum_steps, 1)
                    after(dve, sum_steps, i * (2 * PAIR) + (2 * n + 2))
                    after(dve, pv_multiplied, unit_count(i, units_before(n - 3) - 1))
                    nc.vector.tensor_tensor(probs[:, n % 4, 0:keys * H].rearrange("p (m h) -> p m h", h=H), e,
                                            inv_sum[:, :].unsqueeze(1).broadcast_to([P, keys, H]),
                                            ALU.mult).then_inc(probs_ready, 1)
                if live(i, j, L_QK):
                    n = j - L_QK
                    keys = PROMPT if n % N < PROMPT else N
                    for u, m0 in row_units(n)[1:]:
                        scores_of_unit(i, n, u, m0)
                    sc = scores[:, 0:keys * H].rearrange("p (m h) -> p m h", h=H)
                    after(dve, qk_reduced, unit_count(i, row_units(n)[-1][0]))
                    nc.vector.tensor_reduce(row_max[:, :], sc.rearrange("p m h -> p h m"), AX_X,
                                            ALU.max).then_inc(max_ready, 1)
                    after(dve, max_ready, tile_count(i, n))
                    after(dve, exps_ready, tile_count(i, n - 1))
                    nc.vector.tensor_tensor(shifted[:, 0:keys * H].rearrange("p (m h) -> p m h", h=H), sc,
                                            row_max[:, :].unsqueeze(1).broadcast_to([P, keys, H]),
                                            ALU.subtract).then_inc(shifted_ready, 1)

            run_slots(dve, slot)


_INS = ['L0_attn_x', 'L0_attn_Wqkv', 'L0_attn_bqkv', 'L0_attn_Wproj', 'L0_attn_bproj', 'L0_ffn_weight', 'L0_ffn_bias']


def kernel(**inputs):
    import numpy as np
    import concourse.bacc as bacc
    from concourse.bass_utils import run_bass_kernel_spmd

    nc = bacc.Bacc("TRN2", target_bir_lowering=False, num_devices=1)
    arrays, args = {}, []
    for name in _INS:
        a = np.ascontiguousarray(inputs[name])
        arrays[f"in_{name}"] = a
        args.append(nc.dram_tensor(f"in_{name}", a.shape, mybir.dt.from_np(a.dtype), kind="ExternalInput").ap())
    shape = inputs['L0_attn_x'].shape
    args.append(nc.dram_tensor("out", shape, F32, kind="ExternalOutput").ap())
    attention_and_fp8_linear(nc, *args)
    r = run_bass_kernel_spmd(nc, [arrays], core_ids=[0])
    return r.results[0]["out"]
```

```python
from contextlib import ExitStack

import concourse.bass as bass
from concourse import mybir

F32 = mybir.dt.float32
F16 = mybir.dt.float16
BF16 = mybir.dt.bfloat16
FP8 = mybir.dt.float8e4
I32 = mybir.dt.int32
ALU = mybir.AluOpType
ACT = mybir.ActivationFunctionType
AX_X = mybir.AxisListType.X

P = 128
N = 8
B = 2048
C = 512
H = 16
D = C // H
KC = C // P
QKV = 3 * C
EPS = 1e-5
PROMPT = 4
TILES = N * B // P
QK_SHARED = 5
PV_SHARED = 5
PAIR = 2 * N
QUAD = 4 * C
UNITS = 12
FP8_MAX = 448.0
CHIP_FP8_MAX = 240.0

L_STATS, L_NORM, L_TRANS, L_KV, L_RES, L_Q, L_QK, L_SOFT, L_PV, L_SUM, L_PROJ, L_OUT, L_STORE = \
    2, 3, 4, 5, 6, 8, 9, 10, 12, 13, 14, 15, 15


def units_before(n):
    g, r = n // N, n % N
    return UNITS * g + r + max(0, r - 4)


def row_units(n):
    return [(units_before(n) + q, 4 * q) for q in range(1 if n % N < PROMPT else 2)]


def tile_count(i, n):
    return i * PAIR + (n + 1)


def unit_count(i, u):
    return i * (2 * UNITS) + (u + 1)


def after(eng, sem, count):
    if not isinstance(count, int) or count > 0:
        eng.wait_ge(sem, count)


def live(i, j, lag):
    return not isinstance(i, int) or 0 <= i * PAIR + j - lag < TILES


def last_group(i, n):
    return isinstance(i, int) and i * PAIR + n >= TILES - N


def shared(i, n, first):
    return last_group(i, n) and n % N >= first


def own_units(i, u, first):
    if not isinstance(i, int):
        return unit_count(i, u)
    others = sum(1 for n in range(-N, 0) if i * PAIR + n >= 0 and shared(i, n, first) and row_units(n)[1][0] <= u)
    return unit_count(i, u) - others


def row_of(u):
    return next(n for n in range(-3 * N, N) if u in [v for v, _ in row_units(n)])


def run_slots(eng, slot):
    for j in range(PAIR):
        slot(0, j)
    with eng.Fori(1, TILES // PAIR) as i:
        for j in range(PAIR):
            slot(i, j)
    for j in range(PAIR):
        slot(TILES // PAIR, j)


def attention_and_fp8_linear(nc, x, Wqkv, bqkv, Wproj, bproj, Wffn, bffn, out):
    x_v = x.rearrange("n (i two b) c -> n i two b c", two=2, b=P)
    out_v = out.rearrange("n (i two b) c -> n i two b c", two=2, b=P)

    with ExitStack() as ctx:
        def sb(name, shape, dt):
            return ctx.enter_context(nc.sbuf_tensor(name, shape, dt))

        def bank(name):
            return ctx.enter_context(nc.psum_tensor(name, [P, 512], F32))

        def sem(name):
            return ctx.enter_context(nc.semaphore(name))

        wqkv_hi = sb("wqkv_hi", [P, KC, QKV], F16)
        wqkv_lo = sb("wqkv_lo", [P, KC, QKV], F16)
        wproj_hi = sb("wproj_hi", [P, KC, C], F16)
        wproj_lo = sb("wproj_lo", [P, KC, C], F16)
        wffn_q = sb("wffn_q", [P, KC, C], BF16)
        bias_rows = sb("bias_rows", [P, C], BF16)
        k_bias = sb("k_bias", [P, C], F32)
        v_bias_col = sb("v_bias_col", [P, KC], F32)
        ones = sb("ones", [P, P], BF16)
        ident = sb("ident", [P, P], F32)
        out_bias = sb("out_bias", [P, C], F32)
        amax = sb("amax", [P, 8], F32)
        scale = sb("scale", [P, 2], F32)
        unscale = sb("unscale", [P, 2], F32)
        exponent = sb("exponent", [P, 2], I32)
        exp_scale = sb("exp_scale", [P, 1], F32)
        out_scale = sb("out_scale", [P, 1], F32)
        minus_half = sb("minus_half", [P, 1], F32)

        xs = sb("xs", [P, PAIR, C], F32)
        stats = sb("stats", [P, 6], F32)
        mean_var = sb("mean_var", [P, 2, 2], F32)
        minus_mean = sb("minus_mean", [P, 1], F32)
        var_eps = sb("var_eps", [P, 1], F32)
        rstd = sb("rstd", [P, 1], F32)
        xn = sb("xn", [P, C], F32)
        xT_hi = sb("xT_hi", [P, N, C], F16)
        xT_lo = sb("xT_lo", [P, N, C], F16)
        xT_q = sb("xT_q", [P, 2, C], FP8)
        kv = sb("kv", [P, 2, 2, N, C], F32)
        linear16 = sb("linear16", [P, 2, C], F16)
        prod_qk = sb("prod_qk", [P, QUAD], F32)
        scores = sb("scores", [P, N * H], F32)
        row_max = sb("row_max", [P, H], F32)
        shifted = sb("shifted", [P, N * H], F32)
        exps = sb("exps", [P, 4, N * H], F32)
        row_sum = sb("row_sum", [P, H], F32)
        inv_sum = sb("inv_sum", [P, 4, H], F32)
        probs = sb("probs", [P, 2, N * H], F32)
        prod_pv = sb("prod_pv", [P, 2, QUAD], F32)
        halves = sb("halves", [P, 4, QUAD // 2], F32)
        oT_hi = sb("oT_hi", [P, C], F16)
        oT_lo = sb("oT_lo", [P, C], F16)
        projected = sb("projected", [P, C], F32)

        xT_ps, oT_ps, k_ps, v_ps, lin_ps, proj_ps = (
            bank(n) for n in ("xT_ps", "oT_ps", "k_ps", "v_ps", "lin_ps", "proj_ps"))
        q_ps = (bank("q_ps0"), bank("q_ps1"))

        scratch = kv[:, :, :, :, :].rearrange("p a b m c -> p (a b m c)")
        wqkv_nat = scratch[:, 0:6144].rearrange("p (j c) -> p j c", c=C)
        wproj_nat = scratch[:, 6144:8192].rearrange("p (j c) -> p j c", c=C)
        wffn_nat = scratch[:, 8192:10240]
        clipped = scratch[:, 10240:12288]
        half_w = scratch[:, 12288:14336]
        q_small = scratch[:, 14336:14848].bitcast(FP8)
        q_half_small = scratch[:, 14848:15360].bitcast(FP8)
        q_half = scratch[:, 15360:15872].bitcast(FP8)
        diagonals = scratch[:, 15872:16064].bitcast(BF16).rearrange("p (a n) -> p a n", n=P)
        bqkv_nat = halves[:, 3, 0:QKV // P]
        bias_row = prod_pv[0:1, 0, 0:C]
        bias_rest = prod_pv[0:1, 1, 0:C]
        bias_mid = halves[0:1, 0, 0:C // 2].bitcast(BF16)
        bias_low = halves[0:1, 1, 0:C // 2].bitcast(BF16)
        bffn_all = halves[:, 2, 0:C]

        late_prod_qk = scratch[:, 0:QUAD]
        late_prod_pv = scratch[:, 2 * N * C:2 * N * C + 2 * QUAD].rearrange("p (a c) -> p a c", c=QUAD)
        late_q = xn

        def o_buffers(i, n):
            if last_group(i, n):
                return (oT_ps, xT_ps)[n % 2], xT_hi[:, n % 2, :], xT_lo[:, n % 2, :]
            return oT_ps, oT_hi, oT_lo

        def wait_for_o_split(eng, i, n):
            if not last_group(i, n):
                after(eng, proj_summed, tile_count(i, n - 1))
            elif n % N < 2:
                eng.wait_ge(q_summed, tile_count(i, n))
            else:
                eng.wait_ge(proj_summed, tile_count(i, n - 2))

        def pv_place(i, n, u):
            if last_group(i, n) and u % 4 >= 2:
                return late_prod_pv[:, u % 2, :]
            return prod_pv[:, u % 2, :]

        wk_loaded = sem("wk_loaded")
        wv_loaded = sem("wv_loaded")
        wq_loaded = sem("wq_loaded")
        wproj_loaded = sem("wproj_loaded")
        wffn_loaded = sem("wffn_loaded")
        bqkv_loaded = sem("bqkv_loaded")
        biases_loaded = sem("biases_loaded")
        bias_row_loaded = sem("bias_row_loaded")
        consts_set = sem("consts_set")
        ident_ready = sem("ident_ready")
        amax_steps = sem("amax_steps")
        amax_parts = sem("amax_parts")
        amax_ready = sem("amax_ready")
        scale_steps = sem("scale_steps")
        scales_ready = sem("scales_ready")
        bias_steps = sem("bias_steps")
        bias_split = sem("bias_split")
        bias_moved = sem("bias_moved")
        k_bias_loaded = sem("k_bias_loaded")
        k_bias_ready = sem("k_bias_ready")
        v_bias_loaded = sem("v_bias_loaded")
        v_bias_split = sem("v_bias_split")
        v_bias_projected = sem("v_bias_projected")
        biases_added = sem("biases_added")
        out_bias_ready = sem("out_bias_ready")
        wffn_clipped = sem("wffn_clipped")
        wffn_halved = sem("wffn_halved")
        q_half_ready = sem("q_half_ready")
        small_ready = sem("small_ready")
        diagonals_ready = sem("diagonals_ready")
        wffn_transposed = sem("wffn_transposed")
        wffn_ready = sem("wffn_ready")
        w_transposed = sem("w_transposed")
        w_hi_ready = sem("w_hi_ready")
        w_ready = sem("w_ready")

        x_loaded = [sem(f"x_loaded{k}") for k in range(PAIR)]
        y_stored = [sem(f"y_stored{k}") for k in range(PAIR)]
        stats_ready = sem("stats_ready")
        mean_var_ready = sem("mean_var_ready")
        minus_mean_ready = sem("minus_mean_ready")
        centred_ready = sem("centred_ready")
        var_ready = sem("var_ready")
        rstd_ready = sem("rstd_ready")
        xn_ready = sem("xn_ready")
        xT_ready = sem("xT_ready")
        x_hi_q_ready = sem("x_hi_q_ready")
        x_lo_ready = sem("x_lo_ready")
        q_summed, k_summed, v_summed, lin_summed = (
            sem(n) for n in ("q_summed", "k_summed", "v_summed", "lin_summed"))
        k_copied, k_kept, v_kept, lin_rounded = (
            sem(n) for n in ("k_copied", "k_kept", "v_kept", "lin_rounded"))
        res_step = sem("res_step")
        res_ready = sem("res_ready")
        qk_multiplied = sem("qk_multiplied")
        qk_reduced = sem("qk_reduced")
        max_ready = sem("max_ready")
        shifted_ready = sem("shifted_ready")
        exps_ready = sem("exps_ready")
        sum_steps = sem("sum_steps")
        probs_ready = sem("probs_ready")
        pv_multiplied = sem("pv_multiplied")
        pv_halved = sem("pv_halved")
        pv_summed = sem("pv_summed")
        oT_ready = sem("oT_ready")
        o_hi_ready = sem("o_hi_ready")
        o_lo_ready = sem("o_lo_ready")
        proj_summed = sem("proj_summed")
        proj_scaled = sem("proj_scaled")
        late_q_ready = sem("late_q_ready")
        late_qk_multiplied = sem("late_qk_multiplied")
        late_pv_multiplied = sem("late_pv_multiplied")
        late_pv_halved = sem("late_pv_halved")
        y_ready = sem("y_ready")

        banks = (lin_ps, proj_ps, k_ps, v_ps, xT_ps, oT_ps, *q_ps)
        N_PARTS = 4 * KC

        def part_bank(w):
            return banks[(KC + w) % len(banks)]

        def part_place(w):
            what, c = w // KC, w % KC
            if what == 3:
                return wproj_hi, wproj_lo, c, 0, 1
            return wqkv_hi, wqkv_lo, c, (C, 2 * C, 0)[what], 0

        block = ctx.enter_context(nc.Block())

        def wait_for_pv_place(eng, i, n, u, m0):
            after(eng, v_kept, tile_count(i, N * (n // N) + m0 + 3))
            if not last_group(i, n):
                after(eng, pv_halved, unit_count(i, u - 2))
            elif n % N < 2:
                eng.wait_ge(pv_halved, unit_count(i, u - 2))
            elif n % N < 4:
                eng.wait_ge(pv_multiplied, unit_count(i, -UNITS - 1))
            else:
                eng.wait_ge(oT_ready, tile_count(i, row_of(u - 4)))

        def multiply_values(engine, i, n, u, m0):
            v = kv[:, 1, (n // N) % 2, m0:m0 + 4, :].rearrange("p m (h d) -> p (m h) d", d=D)
            p = probs[:, n % 2, m0 * H:(m0 + 4) * H].unsqueeze(2).broadcast_to([P, 4 * H, D])
            o = pv_place(i, n, u).rearrange("p (a d) -> p a d", d=D)
            return engine.tensor_tensor(o, v, p, ALU.mult)

        def halve(engine, i, n, u):
            products = pv_place(i, n, u)
            return engine.tensor_tensor(halves[:, u % 4, :], products[:, 0:QUAD // 2], products[:, QUAD // 2:QUAD], ALU.add)

        def late_halved(i, n):
            return unit_count(i, -UNITS - 1) + sum(1 if r >= PV_SHARED else 2 for r in range(4, n % N + 1))

        def wait_for_late_half(eng, i, n, u):
            eng.wait_ge(oT_ready, tile_count(i, max(-N - 1, row_of(u - 4))))

        @block.sync
        def _(sp):
            sp.dma_start(wffn_nat.rearrange("p (j c) -> p j c", c=C),
                         Wffn.rearrange("(j p) c -> p j c", p=P)).then_inc(wffn_loaded, 16)
            Wqkv_v = Wqkv.rearrange("(j p) c -> p j c", p=P)
            sp.dma_start(wqkv_nat[:, KC:2 * KC], Wqkv_v[:, KC:2 * KC]).then_inc(wk_loaded, 16)
            sp.dma_start(wqkv_nat[:, 2 * KC:3 * KC], Wqkv_v[:, 2 * KC:3 * KC]).then_inc(wv_loaded, 16)
            sp.dma_start(wqkv_nat[:, 0:KC], Wqkv_v[:, 0:KC]).then_inc(wq_loaded, 16)
            sp.dma_start(wproj_nat, Wproj.rearrange("(j p) c -> p j c", p=P)).then_inc(wproj_loaded, 16)
            sp.dma_start(bqkv_nat, bqkv.rearrange("(p j) -> p j", p=P)).then_inc(bqkv_loaded, 16)
            sp.dma_start(bias_row, bqkv[0:C].rearrange("(a n) -> a n", a=1)).then_inc(bias_row_loaded, 16)
            sp.dma_start(k_bias[:, :], bqkv[C:2 * C].partition_broadcast(P)).then_inc(k_bias_loaded, 16)
            with nc.allow_non_contiguous_dma(reason="512 numbers, once"):
                sp.dma_start(v_bias_col[:, :], bqkv[2 * C:3 * C].rearrange("(k p) -> p k", p=P)).then_inc(v_bias_loaded, 16)
            sp.dma_start(out_bias[:, :], bproj.partition_broadcast(P)).then_inc(biases_loaded, 16)
            sp.dma_start(bffn_all, bffn.partition_broadcast(P)).then_inc(biases_loaded, 16)

            def slot(i, j):
                if isinstance(i, int) and (i, j) == (0, L_RES):
                    sp.wait_ge(bias_split, 1)
                    sp.dma_start(bias_rows[1:2, :], bias_mid).then_inc(bias_moved, 16)
                    sp.dma_start(bias_rows[2:3, :], bias_low).then_inc(bias_moved, 16)
                if live(i, j, 0):
                    after(sp, y_stored[j], i * 16)
                    sp.dma_start(xs[:, j, :], x_v[j % N, i, j // N]).then_inc(x_loaded[j], 16)
                if live(i, j, L_STORE):
                    n = j - L_STORE
                    after(sp, y_ready, tile_count(i, n))
                    sp.dma_start(out_v[n % N, i + n // PAIR, (n // N) % 2],
                                 xs[:, n % PAIR, :]).then_inc(y_stored[n % PAIR], 16)

            run_slots(sp, slot)
            for k in range(PAIR):
                sp.wait_ge(y_stored[k], 16 * (TILES // PAIR))

        @block.gpsimd
        def _(pool):
            nc.gpsimd.memset(ident[:, :], 0.0).then_inc(consts_set, 1)
            pool.wait_ge(consts_set, 1)
            nc.gpsimd.affine_select(out=ident[:, :], in_=ident[:, :], compare_op=ALU.not_equal, fill=1.0,
                                    base=0, pattern=[[-1, P]], channel_multiplier=1).then_inc(ident_ready, 1)
            nc.gpsimd.memset(ones[:, :], 1.0).then_inc(consts_set, 1)
            nc.gpsimd.memset(minus_half[:, :], -0.5).then_inc(consts_set, 1)
            nc.gpsimd.memset(bias_rows[:, :], 0.0).then_inc(consts_set, 1)
            pool.wait_ge(amax_parts, 1)
            nc.gpsimd.partition_all_reduce(amax[:, 6:8], amax[:, 4:6], P,
                                           bass.bass_isa.ReduceOp.max).then_inc(amax_ready, 1)
            pool.wait_ge(scales_ready, 1)
            pool.wait_ge(k_bias_loaded, 16)
            nc.gpsimd.tensor_scalar(k_bias[:, :], k_bias[:, :], scale[:, 0:1], 1.0, ALU.mult, ALU.mult).then_inc(k_bias_ready, 1)
            pool.wait_ge(biases_loaded, 32)
            nc.gpsimd.tensor_tensor(out_bias[:, :], out_bias[:, :], bffn_all, ALU.add).then_inc(biases_added, 1)

            def slot(i, j):
                if isinstance(i, int) and (i, j) == (0, L_KV):
                    pool.wait_ge(bias_row_loaded, 16)
                    pool.wait_ge(consts_set, 4)
                    nc.gpsimd.tensor_scalar(bias_row, bias_row, scale[0:1, 0:1], 1.0, ALU.mult, ALU.mult).then_inc(bias_steps, 1)
                    pool.wait_ge(bias_steps, 1)
                    nc.gpsimd.tensor_copy(bias_rows[0:1, :], bias_row).then_inc(bias_steps, 1)
                    pool.wait_ge(bias_steps, 2)
                    nc.gpsimd.tensor_tensor(bias_rest, bias_row, bias_rows[0:1, :], ALU.subtract).then_inc(bias_steps, 1)
                    pool.wait_ge(bias_steps, 3)
                    nc.gpsimd.tensor_copy(bias_mid, bias_rest).then_inc(bias_steps, 1)
                    pool.wait_ge(bias_steps, 4)
                    nc.gpsimd.tensor_tensor(bias_rest, bias_rest, bias_mid, ALU.subtract).then_inc(bias_steps, 1)
                    pool.wait_ge(bias_steps, 5)
                    nc.gpsimd.tensor_copy(bias_low, bias_rest).then_inc(bias_split, 1)
                if live(i, j, L_RES):
                    n = j - L_RES
                    xt = xs[:, n % PAIR, :]
                    if isinstance(i, int) and (i, n) == (0, 0):
                        pool.wait_ge(out_bias_ready, 1)
                    after(pool, centred_ready, tile_count(i, n))
                    nc.gpsimd.tensor_tensor(xt, xt, out_bias[:, :], ALU.add).then_inc(res_step, 1)
                    after(pool, res_step, tile_count(i, n))
                    after(pool, lin_rounded, tile_count(i, n))
                    nc.gpsimd.tensor_tensor(xt, xt, linear16[:, n % 2, :], ALU.add).then_inc(res_ready, 1)
                if live(i, j, L_QK) and shared(i, j - L_QK, QK_SHARED):
                    n = j - L_QK
                    u, m0 = row_units(n)[1]
                    pool.wait_ge(late_q_ready, n % N - QK_SHARED + 1)
                    pool.wait_ge(k_kept, tile_count(i, N * (n // N) + m0 + 3))
                    pool.wait_ge(qk_reduced, unit_count(i, u - 2))
                    nc.gpsimd.tensor_tensor(late_prod_qk.rearrange("p (m c) -> p m c", c=C),
                                            late_q[:, :].unsqueeze(1).broadcast_to([P, 4, C]),
                                            kv[:, 0, (n // N) % 2, m0:m0 + 4, :], ALU.mult).then_inc(late_qk_multiplied, 1)
                if live(i, j, L_OUT) and not last_group(i, j - L_OUT):
                    n = j - L_OUT
                    xt = xs[:, n % PAIR, :]
                    after(pool, proj_scaled, tile_count(i, n))
                    after(pool, res_ready, tile_count(i, n))
                    nc.gpsimd.tensor_tensor(xt, xt, projected[:, :], ALU.add).then_inc(y_ready, 1)
                if live(i, j, L_NORM):
                    n = j - L_NORM
                    after(pool, var_ready, tile_count(i, n))
                    after(pool, xn_ready, tile_count(i, n - 1))
                    nc.gpsimd.tensor_tensor(rstd[:, :], var_eps[:, :], minus_half[:, :],
                                            ALU.pow).then_inc(rstd_ready, 1)
                if live(i, j, L_KV):
                    n = j - L_KV
                    k = kv[:, 0, (n // N) % 2, n % N, :]
                    if isinstance(i, int) and (i, n) == (0, 0):
                        pool.wait_ge(k_bias_ready, 1)
                    after(pool, k_copied, tile_count(i, n))
                    nc.gpsimd.tensor_tensor(k, k, k_bias[:, :], ALU.add).then_inc(k_kept, 1)

                if live(i, j, L_PV):
                    n = j - L_PV
                    keys = PROMPT if n % N < PROMPT else N
                    after(pool, sum_steps, i * (2 * PAIR) + (2 * n + 2))
                    after(pool, pv_multiplied, own_units(i, units_before(n - 1) - 1, PV_SHARED))
                    if shared(i, n - 2, PV_SHARED):
                        pool.wait_ge(late_pv_multiplied, (n - 2) % N - PV_SHARED + 1)
                    nc.gpsimd.tensor_tensor(probs[:, n % 2, 0:keys * H].rearrange("p (m h) -> p m h", h=H),
                                            exps[:, n % 4, 0:keys * H].rearrange("p (m h) -> p m h", h=H),
                                            inv_sum[:, n % 4, :].unsqueeze(1).broadcast_to([P, keys, H]),
                                            ALU.mult).then_inc(probs_ready, 1)
                    for u, m0 in row_units(n)[:1 if shared(i, n, PV_SHARED) else 2]:
                        after(pool, probs_ready, tile_count(i, n))
                        wait_for_pv_place(pool, i, n, u, m0)
                        multiply_values(nc.gpsimd, i, n, u, m0).then_inc(pv_multiplied, 1)
                        if shared(i, n, PV_SHARED):
                            pool.wait_ge(pv_multiplied, own_units(i, u, PV_SHARED))
                            wait_for_late_half(pool, i, n, u)
                            halve(nc.gpsimd, i, n, u).then_inc(late_pv_halved, 1)
            run_slots(pool, slot)

        @block.scalar
        def _(act):
            act.wait_ge(ident_ready, 1)
            for a, factor in enumerate((1.0, 2.0, -2.0)):
                nc.scalar.activation(diagonals[:, a, :], ident[:, :], ACT.Copy, scale=factor).then_inc(diagonals_ready, 1)
            act.wait_ge(wffn_clipped, 1)
            nc.scalar.activation(q_small, clipped, ACT.Copy, saturate=False).then_inc(small_ready, 1)
            nc.scalar.activation(q_half_small, clipped, ACT.Copy, scale=0.5, saturate=False).then_inc(small_ready, 1)
            for c in range(KC):
                act.wait_ge(wffn_transposed, c + 1)
                nc.scalar.activation(wffn_q[:, c, :], banks[c][:, :], ACT.Copy).then_inc(wffn_ready, 1)
            act.wait_ge(scales_ready, 1)
            def high_parts(first, last):
                for w in range(first, last):
                    hi, _, c, col, which = part_place(w)
                    act.wait_ge(w_transposed, w + 1)
                    nc.scalar.activation(hi[:, c, col:col + 512], part_bank(w)[:, :], ACT.Copy,
                                         scale=scale[:, which:which + 1]).then_inc(w_hi_ready, 1)

            high_parts(0, 2 * KC)

            def slot(i, j):
                if isinstance(i, int) and (i, j) == (0, L_TRANS):
                    high_parts(2 * KC, N_PARTS)
                if live(i, j, L_QK) and shared(i, j - L_QK, QK_SHARED):
                    n = j - L_QK
                    act.wait_ge(q_summed, tile_count(i, n))
                    act.wait_ge(xT_ready, tile_count(i, -1))
                    after(act, late_qk_multiplied, n % N - QK_SHARED)
                    nc.scalar.activation(late_q[:, :], q_ps[n % 2][:, :], ACT.Copy).then_inc(late_q_ready, 1)
                if live(i, j, L_TRANS):
                    n = j - L_TRANS
                    after(act, xT_ready, tile_count(i, n))
                    after(act, q_summed, tile_count(i, n - N))
                    after(act, lin_summed, tile_count(i, n - 2))
                    nc.scalar.activation(xT_hi[:, n % N, :], xT_ps[:, :], ACT.Copy)
                    nc.scalar.activation(xT_q[:, n % 2, :], xT_ps[:, :], ACT.Copy,
                                         saturate=False).then_inc(x_hi_q_ready, 1)
                if live(i, j, L_PROJ):
                    n = j - L_PROJ
                    after(act, oT_ready, tile_count(i, n))
                    wait_for_o_split(act, i, n)
                    o_ps, o_hi, _ = o_buffers(i, n)
                    nc.scalar.activation(o_hi[:, :], o_ps[:, :], ACT.Copy).then_inc(o_hi_ready, 1)
                if live(i, j, L_OUT) and not last_group(i, j - L_OUT):
                    n = j - L_OUT
                    after(act, proj_summed, tile_count(i, n))
                    after(act, y_ready, tile_count(i, n - 1))
                    nc.scalar.activation(projected[:, :], proj_ps[:, :], ACT.Copy,
                                         scale=out_scale[:, 0:1]).then_inc(proj_scaled, 1)
                if live(i, j, L_NORM):
                    n = j - L_NORM
                    r = n % 2
                    after(act, mean_var_ready, tile_count(i, n))
                    after(act, rstd_ready, tile_count(i, n - 1))
                    nc.scalar.activation(var_eps[:, :], mean_var[:, r, 1:2], ACT.Copy, bias=EPS).then_inc(var_ready, 1)
                    after(act, centred_ready, tile_count(i, n - 1))
                    nc.scalar.activation(minus_mean[:, :], mean_var[:, r, 0:1], ACT.Copy,
                                         scale=-1.0).then_inc(minus_mean_ready, 1)
                if live(i, j, L_KV):
                    n = j - L_KV
                    g = n // N
                    after(act, k_summed, tile_count(i, n))
                    after(act, qk_multiplied, unit_count(i, UNITS * (g - 1) - 1))
                    nc.scalar.activation(kv[:, 0, g % 2, n % N, :], k_ps[:, :], ACT.Copy).then_inc(k_copied, 1)
                if live(i, j, L_NORM):
                    n = j - L_NORM
                    after(act, minus_mean_ready, tile_count(i, n))
                    after(act, xT_ready, tile_count(i, n - 1))
                    nc.scalar.activation(xn[:, :], xs[:, n % PAIR, :], ACT.Identity,
                                         bias=minus_mean[:, 0:1]).then_inc(centred_ready, 1)
                if live(i, j, L_KV):
                    after(act, v_summed, tile_count(i, n := j - L_KV))
                    after(act, pv_multiplied, unit_count(i, UNITS * (n // N - 1) - 1))
                    nc.scalar.activation(kv[:, 1, (n // N) % 2, n % N, :], v_ps[:, :], ACT.Copy).then_inc(v_kept, 1)
                if live(i, j, L_SOFT):
                    n = j - L_SOFT
                    keys = PROMPT if n % N < PROMPT else N
                    after(act, shifted_ready, tile_count(i, n))
                    after(act, probs_ready, tile_count(i, n - 4))
                    nc.scalar.activation(exps[:, n % 4, 0:keys * H], shifted[:, 0:keys * H], ACT.Exp,
                                         scale=exp_scale[:, 0:1]).then_inc(exps_ready, 1)
                if live(i, j, L_NORM):
                    n = j - L_NORM
                    after(act, centred_ready, tile_count(i, n))
                    after(act, rstd_ready, tile_count(i, n))
                    nc.scalar.activation(xn[:, :], xn[:, :], ACT.Copy,
                                         scale=rstd[:, 0:1]).then_inc(xn_ready, 1)
                if live(i, j, L_KV):
                    n = j - L_KV
                    after(act, lin_summed, tile_count(i, n))
                    after(act, res_ready, tile_count(i, n - 2))
                    nc.scalar.activation(linear16[:, n % 2, :], lin_ps[:, :], ACT.Copy).then_inc(lin_rounded, 1)

            run_slots(act, slot)

        @block.tensor
        def _(pe):
            pe.wait_ge(ident_ready, 1)
            pe.wait_ge(diagonals_ready, 3)
            pe.wait_ge(small_ready, 2)
            pe.wait_ge(q_half_ready, 1)
            for c in range(KC):
                for o in range(KC):
                    src = slice(o * C + c * P, o * C + (c + 1) * P)
                    for a, part in enumerate((q_small, q_half, q_half_small)):
                        last = nc.tensor.matmul(banks[c][:, o * P:(o + 1) * P], part[:, src], diagonals[:, a, :],
                                                start=a == 0, stop=a == 2)
                last.then_inc(wffn_transposed, 1)
            for w in range(N_PARTS):
                _, _, c, col, which = part_place(w)
                if w % KC == 0:
                    pe.wait_ge((wk_loaded, wv_loaded, wq_loaded, wproj_loaded)[w // KC], 16)
                if len(banks) - KC <= w < len(banks):
                    pe.wait_ge(wffn_ready, w - (len(banks) - KC) + 1)
                if w >= len(banks):
                    pe.wait_ge(w_ready, w - len(banks) + 1)
                for o in range(4):
                    nat = wproj_nat[:, o, :] if which else wqkv_nat[:, col // P + o, :]
                    last = nc.tensor.transpose(part_bank(w)[:, o * P:(o + 1) * P], nat[:, c * P:(c + 1) * P],
                                               ident[:, :])
                last.then_inc(w_transposed, 1)
            def split_products(acc, t_hi, t_lo, w_hi, w_lo, col, first=True):
                parts = [(t, w, c) for c in range(KC) for t, w in ((t_hi, w_hi), (t_hi, w_lo))]
                parts += [(t_lo, w_hi, c) for c in range(KC)]
                for k, (t, w, c) in enumerate(parts):
                    last = nc.tensor.matmul(acc[:, :], t[:, c * P:(c + 1) * P], w[:, c, col:col + 512],
                                            start=first and k == 0, stop=k == len(parts) - 1)
                return last

            def transpose_o(i, n):
                units = [u for u, _ in row_units(n)]
                if last_group(i, n):
                    if n % N < 4:
                        pe.wait_ge(pv_multiplied, unit_count(i, units[-1]))
                        parts = [pv_place(i, n, u)[:, m * C:(m + 1) * C] for u in units for m in range(4)]
                    else:
                        pe.wait_ge(pv_halved, late_halved(i, n))
                        if shared(i, n, PV_SHARED):
                            pe.wait_ge(late_pv_halved, n % N - PV_SHARED + 1)
                        parts = [halves[:, u % 4, m * C:(m + 1) * C] for u in units for m in range(2)]
                else:
                    after(pe, pv_summed, unit_count(i, units[-1]))
                    parts = [halves[:, u % 4, 0:C] for u in units]
                if last_group(i, n) and n % N == 1:
                    pe.wait_ge(x_lo_ready, tile_count(i, -1))
                elif last_group(i, n) and n % N > 1:
                    pe.wait_ge(o_lo_ready, tile_count(i, n - 2))
                else:
                    after(pe, o_lo_ready, tile_count(i, n - 1))
                for c in range(KC):
                    for k, part in enumerate(parts):
                        last = nc.tensor.matmul(
                            o_buffers(i, n)[0][:, c * P:(c + 1) * P], part[:, c * P:(c + 1) * P],
                            ident[:, :], start=k == 0, stop=k == len(parts) - 1, is_transpose=True)
                last.then_inc(oT_ready, 1)

            def slot(i, j):
                if isinstance(i, int) and (i, j) == (0, L_TRANS):
                    pe.wait_ge(w_ready, len(banks) + 1)
                if isinstance(i, int) and (i, j) == (0, L_KV):
                    pe.wait_ge(w_ready, N_PARTS)
                if isinstance(i, int) and (i, j) == (0, L_RES):
                    pe.wait_ge(v_bias_split, 1)
                    split_products(proj_ps, oT_hi, oT_lo, wproj_hi, wproj_lo, 0).then_inc(v_bias_projected, 1)
                if live(i, j, L_TRANS):
                    n = j - L_TRANS
                    after(pe, xn_ready, tile_count(i, n))
                    after(pe, x_lo_ready, tile_count(i, n - 1))
                    for c in range(KC):
                        last = nc.tensor.transpose(xT_ps[:, c * P:(c + 1) * P], xn[:, c * P:(c + 1) * P],
                                                   ident[:, :])
                    last.then_inc(xT_ready, 1)
                if live(i, j, L_PROJ) and not last_group(i, j - L_PROJ):
                    transpose_o(i, j - L_PROJ)
                if live(i, j, L_PROJ - 1) and last_group(i, j - L_PROJ + 1) and last_group(i, j - L_PROJ):
                    transpose_o(i, j - L_PROJ + 1)
                if live(i, j, L_KV):
                    n = j - L_KV
                    t_hi, t_lo = xT_hi[:, n % N, :], xT_lo[:, n % N, :]
                    after(pe, x_lo_ready, tile_count(i, n))
                    after(pe, k_copied, tile_count(i, n - 1))
                    split_products(k_ps, t_hi, t_lo, wqkv_hi, wqkv_lo, C).then_inc(k_summed, 1)
                    after(pe, v_kept, tile_count(i, n - 1))
                    after(pe, lin_rounded, tile_count(i, n - 1))
                    split_products(v_ps, t_hi, t_lo, wqkv_hi, wqkv_lo, 2 * C).then_inc(v_summed, 1)
                if isinstance(i, int) and (i, j) == (0, L_Q):
                    pe.wait_ge(consts_set, 4)
                    pe.wait_ge(bias_moved, 32)
                if live(i, j, L_Q):
                    n = j - L_Q
                    acc = q_ps[n % 2]
                    after(pe, qk_multiplied, own_units(i, units_before(n - 1) - 1, QK_SHARED))
                    nc.tensor.matmul(acc[:, :], ones[:, :], bias_rows[:, :], start=True, stop=False)
                    split_products(acc, xT_hi[:, n % N, :], xT_lo[:, n % N, :], wqkv_hi, wqkv_lo, 0,
                                   first=False).then_inc(q_summed, 1)
                if live(i, j, L_KV):
                    n = j - L_KV
                    for c in range(KC):
                        last = nc.tensor.matmul(lin_ps[:, :], xT_q[:, n % 2, c * P:(c + 1) * P], wffn_q[:, c, :],
                                                start=c == 0, stop=c == KC - 1)
                    last.then_inc(lin_summed, 1)
                if live(i, j, L_PROJ):
                    n = j - L_PROJ
                    after(pe, o_lo_ready, tile_count(i, n))
                    if last_group(i, n - 1):
                        pe.wait_ge(y_ready, tile_count(i, n - 1))
                    else:
                        after(pe, proj_scaled, tile_count(i, n - 1))
                    _, o_hi, o_lo = o_buffers(i, n)
                    split_products(proj_ps, o_hi, o_lo, wproj_hi, wproj_lo, 0).then_inc(proj_summed, 1)
                if live(i, j, L_PROJ - 1) and last_group(i, j - L_PROJ + 1) and not last_group(i, j - L_PROJ):
                    transpose_o(i, j - L_PROJ + 1)

            run_slots(pe, slot)

        @block.vector
        def _(dve):
            dve.wait_ge(wffn_loaded, 16)
            nc.vector.tensor_scalar(clipped, wffn_nat, CHIP_FP8_MAX, -CHIP_FP8_MAX, ALU.min,
                                    ALU.max).then_inc(wffn_clipped, 1)
            nc.vector.tensor_scalar(half_w, wffn_nat, 0.5, FP8_MAX / 2, ALU.mult, ALU.min).then_inc(wffn_halved, 1)
            dve.wait_ge(wffn_halved, 1)
            nc.vector.tensor_scalar(q_half, half_w, -FP8_MAX / 2, None, ALU.max, saturate=False).then_inc(q_half_ready, 1)
            for a, (loaded, at) in enumerate(((wk_loaded, KC), (wv_loaded, 2 * KC), (wq_loaded, 0))):
                dve.wait_ge(loaded, 16)
                nc.vector.tensor_reduce(amax[:, a:a + 1], wqkv_nat[:, at:at + KC].rearrange("p j c -> p (j c)"),
                                        AX_X, ALU.max, apply_absolute_value=True).then_inc(amax_steps, 1)
            dve.wait_ge(wproj_loaded, 16)
            nc.vector.tensor_reduce(amax[:, 5:6], wproj_nat.rearrange("p j c -> p (j c)"), AX_X, ALU.max,
                                    apply_absolute_value=True).then_inc(amax_steps, 1)
            dve.wait_ge(bqkv_loaded, 16)
            nc.vector.tensor_reduce(amax[:, 3:4], bqkv_nat, AX_X, ALU.max,
                                    apply_absolute_value=True).then_inc(amax_steps, 1)
            dve.wait_ge(amax_steps, 3)
            nc.vector.tensor_reduce(amax[:, 4:5], amax[:, 0:3], AX_X, ALU.max).then_inc(amax_steps, 1)
            dve.wait_ge(amax_steps, 6)
            nc.vector.scalar_tensor_tensor(out=amax[:, 4:5], in0=amax[:, 3:4], scalar=1.0 / 256,
                                           in1=amax[:, 4:5], op0=ALU.mult, op1=ALU.max).then_inc(amax_parts, 1)
            dve.wait_ge(amax_ready, 1)
            nc.vector.tensor_scalar(amax[:, 6:8], amax[:, 6:8], 2.0 ** -100, None, ALU.max).then_inc(scale_steps, 1)
            dve.wait_ge(scale_steps, 1)
            nc.vector.tensor_scalar(exponent[:, :], amax[:, 6:8].bitcast(I32), 0x7F800000, None,
                                    ALU.bitwise_and).then_inc(scale_steps, 1)
            dve.wait_ge(scale_steps, 2)
            nc.vector.tensor_scalar(scale[:, :].bitcast(I32), exponent[:, :], -1.0, 259.0 * 2 ** 23,
                                    ALU.mult, ALU.add).then_inc(scale_steps, 1)
            nc.vector.tensor_scalar(unscale[:, :].bitcast(I32), exponent[:, :], 5.0 * 2 ** 23, None,
                                    ALU.subtract).then_inc(scale_steps, 1)
            dve.wait_ge(scale_steps, 4)
            nc.vector.tensor_tensor(out_scale[:, :], unscale[:, 0:1], unscale[:, 1:2], ALU.mult).then_inc(scale_steps, 1)
            nc.vector.scalar_tensor_tensor(out=exp_scale[:, :], in0=unscale[:, 0:1], scalar=float(D) ** -0.5,
                                           in1=unscale[:, 0:1], op0=ALU.mult, op1=ALU.mult).then_inc(scales_ready, 1)
            def low_parts(first, last):
                for w in range(first, last):
                    hi, lo, c, col, which = part_place(w)
                    dve.wait_ge(w_hi_ready, w + 1)
                    nc.vector.scalar_tensor_tensor(out=lo[:, c, col:col + 512], in0=part_bank(w)[:, :],
                                                   scalar=scale[:, which:which + 1], in1=hi[:, c, col:col + 512],
                                                   op0=ALU.mult, op1=ALU.subtract).then_inc(w_ready, 1)

            low_parts(0, KC)

            def scores_of_unit(i, n, u, m0):
                after(dve, q_summed, tile_count(i, n))
                after(dve, k_kept, tile_count(i, N * (n // N) + m0 + 3))
                if shared(i, n, QK_SHARED):
                    dve.wait_ge(late_q_ready, n % N - QK_SHARED + 1)
                if shared(i, n, QK_SHARED) and m0:
                    dve.wait_ge(late_qk_multiplied, n % N - QK_SHARED + 1)
                    products = late_prod_qk
                else:
                    after(dve, qk_reduced, unit_count(i, u - 1))
                    k = kv[:, 0, (n // N) % 2, m0:m0 + 4, :]
                    qb = q_ps[n % 2][:, :].unsqueeze(1).broadcast_to([P, 4, C])
                    nc.vector.tensor_tensor(prod_qk[:, :].rearrange("p (m c) -> p m c", c=C), qb, k,
                                            ALU.mult).then_inc(qk_multiplied, 1)
                    after(dve, qk_multiplied, own_units(i, u, QK_SHARED))
                    products = prod_qk[:, :]
                after(dve, shifted_ready, tile_count(i, n - 1))
                nc.vector.tensor_reduce(scores[:, m0 * H:(m0 + 4) * H],
                                        products.rearrange("p (a d) -> p a d", d=D), AX_X,
                                        ALU.add).then_inc(qk_reduced, 1)

            def slot(i, j):
                if isinstance(i, int) and (i, j) == (0, L_TRANS):
                    low_parts(KC, N_PARTS)
                if isinstance(i, int) and (i, j) == (0, L_KV):
                    dve.wait_ge(v_bias_loaded, 16)
                    v_bias = v_bias_col[:, :].unsqueeze(2).broadcast_to([P, KC, P])
                    bias_hi = oT_hi[:, :].rearrange("p (k t) -> p k t", t=P)
                    dve.wait_ge(scales_ready, 1)
                    nc.vector.tensor_scalar(bias_hi, v_bias, scale[:, 0:1], None, ALU.mult).then_inc(scale_steps, 1)
                    dve.wait_ge(scale_steps, 6)
                    nc.vector.scalar_tensor_tensor(out=oT_lo[:, :].rearrange("p (k t) -> p k t", t=P), in0=v_bias,
                                                   scalar=scale[:, 0:1], in1=bias_hi,
                                                   op0=ALU.mult, op1=ALU.subtract).then_inc(v_bias_split, 1)
                if isinstance(i, int) and (i, j) == (0, L_RES):
                    dve.wait_ge(v_bias_projected, 1)
                    dve.wait_ge(biases_added, 1)
                    nc.vector.scalar_tensor_tensor(out=out_bias[:, :], in0=proj_ps[:, :], scalar=out_scale[:, 0:1],
                                                   in1=out_bias[:, :], op0=ALU.mult, op1=ALU.add).then_inc(out_bias_ready, 1)
                if live(i, j, L_TRANS):
                    n = j - L_TRANS
                    after(dve, x_hi_q_ready, tile_count(i, n))
                    nc.vector.tensor_tensor(xT_lo[:, n % N, :], xT_ps[:, :], xT_hi[:, n % N, :],
                                            ALU.subtract).then_inc(x_lo_ready, 1)
                if live(i, j, L_PROJ):
                    n = j - L_PROJ
                    after(dve, o_hi_ready, tile_count(i, n))
                    wait_for_o_split(dve, i, n)
                    o_ps, o_hi, o_lo = o_buffers(i, n)
                    nc.vector.tensor_tensor(o_lo[:, :], o_ps[:, :], o_hi[:, :],
                                            ALU.subtract).then_inc(o_lo_ready, 1)
                if live(i, j, L_SUM) and last_group(i, j - L_SUM) and (j - L_SUM) % N >= 4:
                    n = j - L_SUM
                    for u, _ in row_units(n)[1 if shared(i, n, PV_SHARED) else 0:]:
                        if shared(i, n, PV_SHARED):
                            dve.wait_ge(late_pv_multiplied, n % N - PV_SHARED + 1)
                        else:
                            dve.wait_ge(pv_multiplied, own_units(i, u, PV_SHARED))
                        wait_for_late_half(dve, i, n, u)
                        halve(nc.vector, i, n, u).then_inc(pv_halved, 1)
                if live(i, j, L_PV) and shared(i, j - L_PV, PV_SHARED):
                    n = j - L_PV
                    u, m0 = row_units(n)[1]
                    dve.wait_ge(probs_ready, tile_count(i, n))
                    wait_for_pv_place(dve, i, n, u, m0)
                    multiply_values(nc.vector, i, n, u, m0).then_inc(late_pv_multiplied, 1)
                if live(i, j, L_OUT) and last_group(i, j - L_OUT):
                    n = j - L_OUT
                    xt = xs[:, n % PAIR, :]
                    dve.wait_ge(proj_summed, tile_count(i, n))
                    dve.wait_ge(res_ready, tile_count(i, n))
                    dve.wait_ge(y_ready, tile_count(i, n - 1))
                    nc.vector.scalar_tensor_tensor(out=xt, in0=proj_ps[:, :], scalar=out_scale[:, 0:1], in1=xt,
                                                   op0=ALU.mult, op1=ALU.add).then_inc(y_ready, 1)
                if live(i, j, L_SUM) and not last_group(i, j - L_SUM):
                    n = j - L_SUM
                    for u, _ in row_units(n):
                        after(dve, pv_multiplied, unit_count(i, u))
                        after(dve, oT_ready, tile_count(i, n - 4 if n % N < PROMPT else n - 2))
                        halve(nc.vector, i, n, u).then_inc(pv_halved, 1)
                if live(i, j, L_STATS):
                    n = j - L_STATS
                    after(dve, x_loaded[n % PAIR], i * 16 + 16 * (n // PAIR + 1))
                    after(dve, mean_var_ready, tile_count(i, n - 1))
                    nc.vector.bn_stats(stats[:, :], xs[:, n % PAIR, :]).then_inc(stats_ready, 1)
                    after(dve, minus_mean_ready, tile_count(i, n - 2))
                    after(dve, stats_ready, tile_count(i, n))
                if live(i, j, L_SUM) and not last_group(i, j - L_SUM):
                    for u, _ in row_units(j - L_SUM):
                        after(dve, pv_halved, unit_count(i, u))
                        nc.vector.tensor_tensor(halves[:, u % 4, 0:C], halves[:, u % 4, 0:C],
                                                halves[:, u % 4, C:2 * C], ALU.add).then_inc(pv_summed, 1)
                if live(i, j, L_STATS):
                    n = j - L_STATS
                    nc.vector.bn_aggr(mean_var[:, n % 2, :], stats[:, :]).then_inc(mean_var_ready, 1)
                if live(i, j, L_QK):
                    n = j - L_QK
                    scores_of_unit(i, n, *row_units(n)[0])
                if live(i, j, L_SOFT):
                    n = j - L_SOFT
                    keys = PROMPT if n % N < PROMPT else N
                    e = exps[:, n % 4, 0:keys * H].rearrange("p (m h) -> p m h", h=H)
                    after(dve, exps_ready, tile_count(i, n))
                    nc.vector.tensor_reduce(row_sum[:, :], e.rearrange("p m h -> p h m"), AX_X,
                                            ALU.add).then_inc(sum_steps, 1)
                    after(dve, sum_steps, i * (2 * PAIR) + (2 * n + 1))
                    nc.vector.reciprocal(inv_sum[:, n % 4, :], row_sum[:, :]).then_inc(sum_steps, 1)
                if live(i, j, L_QK):
                    n = j - L_QK
                    keys = PROMPT if n % N < PROMPT else N
                    for u, m0 in row_units(n)[1:]:
                        scores_of_unit(i, n, u, m0)
                    sc = scores[:, 0:keys * H].rearrange("p (m h) -> p m h", h=H)
                    after(dve, qk_reduced, unit_count(i, row_units(n)[-1][0]))
                    nc.vector.tensor_reduce(row_max[:, :], sc.rearrange("p m h -> p h m"), AX_X,
                                            ALU.max).then_inc(max_ready, 1)
                    after(dve, max_ready, tile_count(i, n))
                    after(dve, exps_ready, tile_count(i, n - 1))
                    nc.vector.tensor_tensor(shifted[:, 0:keys * H].rearrange("p (m h) -> p m h", h=H), sc,
                                            row_max[:, :].unsqueeze(1).broadcast_to([P, keys, H]),
                                            ALU.subtract).then_inc(shifted_ready, 1)

            run_slots(dve, slot)


_INS = ['L0_attn_x', 'L0_attn_Wqkv', 'L0_attn_bqkv', 'L0_attn_Wproj', 'L0_attn_bproj', 'L0_ffn_weight', 'L0_ffn_bias']


def kernel(**inputs):
    import numpy as np
    import concourse.bacc as bacc
    from concourse.bass_utils import run_bass_kernel_spmd

    nc = bacc.Bacc("TRN2", target_bir_lowering=False, num_devices=1)
    arrays, args = {}, []
    for name in _INS:
        a = np.ascontiguousarray(inputs[name])
        arrays[f"in_{name}"] = a
        args.append(nc.dram_tensor(f"in_{name}", a.shape, mybir.dt.from_np(a.dtype), kind="ExternalInput").ap())
    shape = inputs['L0_attn_x'].shape
    args.append(nc.dram_tensor("out", shape, F32, kind="ExternalOutput").ap())
    attention_and_fp8_linear(nc, *args)
    r = run_bass_kernel_spmd(nc, [arrays], core_ids=[0])
    return r.results[0]["out"]
```
